# Optimizing a Trainium2 kernel written in Bass

```python
import numpy as np
import jax
import jax.numpy as jnp

def _softmax(x, axis=-1):
    return jax.nn.softmax(x, axis=axis)

def _gelu(x):
    return jax.nn.gelu(x, approximate=True)

def _silu(x):
    return jax.nn.silu(x)

def _sigmoid(x):
    return jax.nn.sigmoid(x)

def _layernorm(x, axis=-1, eps=1e-05):
    m = jnp.mean(x, axis=axis, keepdims=True)
    v = jnp.var(x, axis=axis, keepdims=True)
    return (x - m) / jnp.sqrt(v + eps)

def _scatter_add(tgt, idx, src, axis=0):
    return tgt.at[idx].add(src)

def _segment_sum(src, seg, n):
    return jax.ops.segment_sum(src, seg, n)
kernel_name = 'mk_flamingo_gated_d1_seqx_r2_b1d803'

def setup_inputs(seed: int=0):
    np.random.seed(seed)
    _w = jnp.asarray

    def _rec_inputs():
        import jax
        import jax.numpy as jnp
        _rk = jax.random.key(seed)
        x = -0.0002928 + 1 * jax.random.normal(jax.random.fold_in(_rk, 1), (16, 512, 512), jnp.float32)
        _lenS = 512 - jax.random.randint(jax.random.fold_in(_rk, 7), (16,), 0, max(1, 512 // 4) + 1, jnp.int32)
        _lenS2 = 512 - jax.random.randint(jax.random.fold_in(_rk, 8), (16,), 0, max(1, 512 // 4) + 1, jnp.int32)
        _ctx_1024P = jax.random.normal(jax.random.fold_in(_rk, 11), (16, 16, 512), jnp.float32)
        _ctx_1024c = jax.random.dirichlet(jax.random.fold_in(_rk, 511), 0.3 * jnp.ones((16,), jnp.float32), (16, 512))
        _ctx_1024t = jnp.einsum('bsk,bkd->bsd', _ctx_1024c, _ctx_1024P)
        _ctx_1024t = _ctx_1024t * jax.lax.rsqrt(jnp.mean(jnp.square(_ctx_1024t)) + 1e-12) * 0.953939
        ctx_1024 = -1.39393e-06 + 0.999914 * (_ctx_1024t + 0.3 * jax.random.normal(jax.random.fold_in(_rk, 611), (16, 512, 512), jnp.float32))
        _validS = jnp.arange(512)[None, :] < _lenS[:, None]
        _validS2 = jnp.arange(512)[None, :] < _lenS2[:, None]
        _causal = jnp.tril(jnp.ones((512, 512), dtype=bool))
        mask_BxS2_if1 = jnp.where(jnp.ones((16, 512), dtype=bool), 1, 0).astype(jnp.int32)
        _g = jax.random.normal(jax.random.fold_in(_rk, 9001), (2, 1), jnp.float32)
        _g = jnp.sign(_g) * jnp.maximum(jnp.abs(_g), 1.0) + (_g == 0) * 1.0
        g_xattn = _g[0]
        g_ffn = _g[1]
        return (x, ctx_1024, mask_BxS2_if1, g_xattn, g_ffn)
    x, ctx_1024, mask_BxS2_if1, g_xattn, g_ffn = _rec_inputs()

    def _L0_xattn_setup():
        import jax, jax.numpy as jnp
        import numpy as np
        B, S, D, H = (2, 1024, 512, 16)
        DH = D // H
        SCALE = DH ** (-0.5)
        key = jax.random.key(seed)
        ks = jax.random.split(key, 12)
        std = D ** (-0.5)
        return {'Q': jax.random.normal(ks[0], (B, S, D), jnp.float32), 'K': jax.random.normal(ks[1], (B, S, D), jnp.float32), 'V': jax.random.normal(ks[2], (B, S, D), jnp.float32), 'mask': jnp.ones((B, S), jnp.int32), 'Wq': jax.random.normal(ks[3], (D, D), jnp.float32) * std, 'bq': jnp.zeros((D,), jnp.float32), 'Wk': jax.random.normal(ks[4], (D, D), jnp.float32) * std, 'bk': jnp.zeros((D,), jnp.float32), 'Wv': jax.random.normal(ks[5], (D, D), jnp.float32) * std, 'bv': jnp.zeros((D,), jnp.float32), 'Wo': jax.random.normal(ks[6], (D, D), jnp.float32) * std, 'bo': jnp.zeros((D,), jnp.float32)}
    _L0_xattn_all = _L0_xattn_setup()
    _L0_xattn_in = {k: v for k, v in _L0_xattn_all.items() if k in ('Wq', 'bq', 'Wk', 'bk', 'Wv', 'bv', 'Wo', 'bo')}
    del _L0_xattn_all

    def _L0_ffn_setup():
        import jax, jax.numpy as jnp
        import numpy as np
        DIM = 512

        def _reference_tuple_inner(x, W_r, W_k, W_v, mu_r, mu_k):
            B, T, C = x.shape
            x_prev = jnp.concatenate([jnp.zeros((B, 1, C), x.dtype), x[:, :-1, :]], axis=1)
            xr = mu_r * x + (1.0 - mu_r) * x_prev
            xk = mu_k * x + (1.0 - mu_k) * x_prev
            r = jax.nn.sigmoid(jnp.einsum('btc,dc->btd', xr, W_r))
            k = jnp.einsum('btc,dc->btd', xk, W_k)
            k_act = jnp.square(jax.nn.relu(k))
            out = r * jnp.einsum('btc,dc->btd', k_act, W_v)
            new_state = x[:, -1, :]
            return (out, new_state)
        key = jax.random.key(seed)
        ks = jax.random.split(key, 6)
        B, T, C = (8, 1024, DIM)
        x = jax.random.normal(ks[0], (B, T, C), dtype=jnp.float32)
        s = 1.0 / np.sqrt(C)
        W_r = jax.random.uniform(ks[1], (C, C), jnp.float32, -s, s)
        W_k = jax.random.uniform(ks[2], (C, C), jnp.float32, -s, s)
        W_v = jax.random.uniform(ks[3], (C, C), jnp.float32, -s, s)
        mu_r = jax.random.uniform(ks[4], (C,), jnp.float32)
        mu_k = jax.random.uniform(ks[5], (C,), jnp.float32)
        return {'x': x, 'W_r': W_r, 'W_k': W_k, 'W_v': W_v, 'mu_r': mu_r, 'mu_k': mu_k}
    _L0_ffn_all = _L0_ffn_setup()
    _L0_ffn_in = {k: v for k, v in _L0_ffn_all.items() if k in ('W_r', 'W_k', 'W_v', 'mu_r', 'mu_k')}
    del _L0_ffn_all
    return {'x': x, 'ctx_1024': ctx_1024, 'mask_BxS2_if1': mask_BxS2_if1, 'g_xattn': g_xattn, 'g_ffn': g_ffn, 'L0_xattn_Wq': _L0_xattn_in['Wq'], 'L0_xattn_bq': _L0_xattn_in['bq'], 'L0_xattn_Wk': _L0_xattn_in['Wk'], 'L0_xattn_bk': _L0_xattn_in['bk'], 'L0_xattn_Wv': _L0_xattn_in['Wv'], 'L0_xattn_bv': _L0_xattn_in['bv'], 'L0_xattn_Wo': _L0_xattn_in['Wo'], 'L0_xattn_bo': _L0_xattn_in['bo'], 'L0_ffn_W_r': _L0_ffn_in['W_r'], 'L0_ffn_W_k': _L0_ffn_in['W_k'], 'L0_ffn_W_v': _L0_ffn_in['W_v'], 'L0_ffn_mu_r': _L0_ffn_in['mu_r'], 'L0_ffn_mu_k': _L0_ffn_in['mu_k']}

def reference(x, ctx_1024, mask_BxS2_if1, g_xattn, g_ffn, L0_xattn_Wq, L0_xattn_bq, L0_xattn_Wk, L0_xattn_bk, L0_xattn_Wv, L0_xattn_bv, L0_xattn_Wo, L0_xattn_bo, L0_ffn_W_r, L0_ffn_W_k, L0_ffn_W_v, L0_ffn_mu_r, L0_ffn_mu_k):
    import jax
    import jax.numpy as jnp

    def _L0_xattn_ref(Q, K, V, mask, Wq, bq, Wk, bk, Wv, bv, Wo, bo):
        import jax, jax.numpy as jnp
        import numpy as np
        B, S, D, H = (2, 1024, 512, 16)
        DH = D // H
        SCALE = DH ** (-0.5)
        b, s, d = Q.shape
        q = (Q @ Wq.T + bq).reshape(b, s, H, DH).transpose(0, 2, 1, 3)
        k = (K @ Wk.T + bk).reshape(b, s, H, DH).transpose(0, 2, 1, 3)
        v = (V @ Wv.T + bv).reshape(b, s, H, DH).transpose(0, 2, 1, 3)
        scores = jnp.einsum('bhqd,bhkd->bhqk', q, k) * SCALE
        scores = jnp.where(mask[:, None, None, :] == 0, -jnp.inf, scores)
        causal = jnp.arange(s)[:, None] >= jnp.arange(s)[None, :]
        scores = jnp.where(causal[None, None], scores, -jnp.inf)
        attn = jax.nn.softmax(scores, axis=-1)
        out = jnp.einsum('bhqk,bhkd->bhqd', attn, v)
        out = out.transpose(0, 2, 1, 3).reshape(b, s, d)
        return out @ Wo.T + bo

    def _L0_ffn_ref(x, W_r, W_k, W_v, mu_r, mu_k):
        import jax, jax.numpy as jnp
        import numpy as np
        DIM = 512

        def _reference_tuple_inner(x, W_r, W_k, W_v, mu_r, mu_k):
            B, T, C = x.shape
            x_prev = jnp.concatenate([jnp.zeros((B, 1, C), x.dtype), x[:, :-1, :]], axis=1)
            xr = mu_r * x + (1.0 - mu_r) * x_prev
            xk = mu_k * x + (1.0 - mu_k) * x_prev
            r = jax.nn.sigmoid(jnp.einsum('btc,dc->btd', xr, W_r))
            k = jnp.einsum('btc,dc->btd', xk, W_k)
            k_act = jnp.square(jax.nn.relu(k))
            out = r * jnp.einsum('btc,dc->btd', k_act, W_v)
            new_state = x[:, -1, :]
            return (out, new_state)
        return _reference_tuple_inner(x, W_r, W_k, W_v, mu_r, mu_k)[0]
    x = x + jnp.tanh(g_xattn[0]) * _L0_xattn_ref(_layernorm(x, axis=-1), ctx_1024, ctx_1024, mask_BxS2_if1, L0_xattn_Wq, L0_xattn_bq, L0_xattn_Wk, L0_xattn_bk, L0_xattn_Wv, L0_xattn_bv, L0_xattn_Wo, L0_xattn_bo)
    x = x + jnp.tanh(g_ffn[0]) * _L0_ffn_ref(_layernorm(x, axis=-1), L0_ffn_W_r, L0_ffn_W_k, L0_ffn_W_v, L0_ffn_mu_r, L0_ffn_mu_k)
    return x

_drawn_inputs = setup_inputs


def setup_inputs(seed=0):
    import zlib

    import numpy as np

    out = dict(_drawn_inputs(seed))
    spreads = {'L0_xattn_bq': (0.0, 0.507),
     'L0_xattn_bk': (0.0, 0.8),
     'L0_xattn_bv': (0.0, 0.1),
     'L0_xattn_bo': (0.0, 0.1)}
    factors = {'L0_ffn_W_r': 3.358, 'L0_ffn_mu_r': 7.621}
    for name, (base, spread) in spreads.items():
        noise = np.random.default_rng([zlib.crc32(name.encode()), seed]).standard_normal(out[name].shape)
        drawn = base * np.exp(spread * noise) if base else spread * noise
        out[name] = jnp.asarray(drawn.astype(out[name].dtype))
    for name, factor in factors.items():
        out[name] = (out[name] * factor).astype(out[name].dtype)
    return out
```

```python
from contextlib import ExitStack

import numpy as np

import concourse.bass as bass
from concourse import mybir

ALU = mybir.AluOpType
ACT = mybir.ActivationFunctionType
F32 = mybir.dt.float32
F32R = mybir.dt.float32r
I32 = mybir.dt.int32

P = 128
HEADS = 16
LN_EPS = 1e-5
MASKED = -1e30
RSQRT_SEED = float(0x5F3759DF)


def wait(engine, semaphore, count):
    if not isinstance(count, int) or count > 0:
        engine.wait_ge(semaphore, count)


def stand_alone(engine, semaphore, b):
    if not isinstance(b, int):
        engine.sem_inc(semaphore, 1)


def exact_product(nc, out, stationary, moving, steps):
    for n in range(steps):
        (s_high, s_low), (m_high, m_low) = stationary(n), moving(n)
        nc.tensor.matmul(out, s_high, m_high, start=(n == 0), stop=False)
        nc.tensor.matmul(out, s_high, m_low, start=False, stop=False)
        last = nc.tensor.matmul(out, s_low, m_high, start=False, stop=(n == steps - 1))
    return last


def attention_phase(nc, x, ctxT, mask, g_xattn, wqT, bq, wkT, bk, wvT, bv, woT, bo, x1):
    B, S, D = x.shape
    H = HEADS
    DH = D // H
    SCALE = float(DH) ** -0.5
    T = S // P
    K = D // P
    HG = P // DH
    PARTS = P // DH
    assert T == 4 and K == 4 and HG == 4 and PARTS == 4

    SEG = [P * t * (t + 1) // 2 for t in range(T + 1)]
    PT_AT = {0: 0, 1: 512, 3: 896, 2: 1024}
    PT_SETS = [[0], [1, 3], [2]]
    PT_COLS = [(0, 512), (512, 1024), (1024, 1280)]

    with ExitStack() as ctx:
        def sb(name, shape, dt=F32):
            return ctx.enter_context(nc.sbuf_tensor(name, shape, dt))

        def psum(name):
            return ctx.enter_context(nc.psum_tensor(name, [P, 512], F32))

        def sem(name):
            return ctx.enter_context(nc.semaphore(name))

        w = {n: [sb(f"w{n}_{part}", [P, K, D], F32R) for part in ("high", "low")] for n in "qkvo"}
        xT = [sb(f"xT_{part}", [P, K, S], F32R) for part in ("high", "low")]
        cT = [sb(f"cT_{part}", [P, K, S], F32R) for part in ("high", "low")]
        x_io = [sb(f"x_io{n}", [P, D]) for n in range(2)]
        c_in = [sb(f"c_in{n}", [P, S]) for n in range(2)]
        staged = [sb(f"staged_{part}", [P, S], F32R) for part in ("high", "low")]
        q_stack = [sb(f"q_stack{n}", [P, HG, S], F32R) for n in range(2)]
        k_stack = [sb(f"k_stack{n}", [P, HG, S], F32R) for n in range(2)]
        v = sb("v", [P, T, D])
        probs = sb("probs", [P, 2, SEG[T]])
        probsT = sb("probsT", [P, HG, SEG[T]])
        bias = sb("bias", [P, SEG[T]])
        mask_row = sb("mask_row", [P, S])
        attn = [sb(f"attn_{part}", [P, K, S], F32R) for part in ("high", "low")]
        norm = sb("norm", [P, S])
        bo_gated = sb("bo_gated", [P, D])
        ident = sb("ident", [P, P])
        causal = sb("causal", [P, P])
        columns = sb("columns", [P, 3, K])
        gate = sb("gate", [P, 1])
        least = sb("least", [P, K, T, HG])
        sums = sb("sums", [P, K, T, HG])
        live = sb("live", [P, T, HG])
        inverse = sb("inverse", [P, T, HG])
        stats = sb("stats", [P, 6])
        moments = sb("moments", [P, 2, 2])
        rstd = sb("rstd", [P, 2, 1])
        newton = sb("newton", [P, 3])

        score_ps = [psum(f"score_ps{n}") for n in range(2)]
        pt_ps = [psum(f"pt_ps{n}") for n in range(2)]
        proj_ps = [psum(f"proj_ps{n}") for n in range(2)]
        value_ps = psum("value_ps")
        norm_ps = psum("norm_ps")

        w_loaded = {n: sem(f"w{n}_loaded") for n in "qkvo"}
        sp_turns, pool_turns, dve_turns = sem("sp_turns"), sem("pool_turns"), sem("dve_turns")
        w_high = sem("w_high")
        w_low = sem("w_low")
        small_loaded = sem("small_loaded")
        pool_const = sem("pool_const")
        gate_ready = sem("gate_ready")
        x_loaded = [sem(f"x_loaded{n}") for n in range(2)]
        ln_step = sem("ln_step")
        ln_stats = sem("ln_stats")
        ln_applied = sem("ln_applied")
        xt_done = sem("xt_done")
        xt_high = sem("xt_high")
        xt_low = sem("xt_low")
        c_loaded = [sem(f"c_loaded{n}") for n in range(2)]
        c_high = sem("c_high")
        c_low = sem("c_low")
        q_done, k_done, v_done, o_done = (sem(f"{n}_done") for n in "qkvo")
        q_high, k_high = sem("q_high"), sem("k_high")
        q_low, k_low = sem("q_low"), sem("k_low")
        v_copied = sem("v_copied")
        q_stacked = [sem(f"q_stacked{n}") for n in range(2)]
        k_stacked = [sem(f"k_stacked{n}") for n in range(2)]
        mask_loaded = sem("mask_loaded")
        mask_ready = sem("mask_ready")
        bias_ready = sem("bias_ready")
        scores_done = sem("scores_done")
        scores_read = sem("scores_read")
        exp_done = sem("exp_done")
        pt_done = sem("pt_done")
        pt_act = sem("pt_act")
        pt_dve = sem("pt_dve")
        values_done = sem("values_done")
        inv_step = sem("inv_step")
        norm_spread = sem("norm_spread")
        norm_done = sem("norm_done")
        norm_copied = sem("norm_copied")
        normalised = sem("normalised")
        attn_high = sem("attn_high")
        attn_low = sem("attn_low")
        res_loaded = [sem(f"res_loaded{n}") for n in range(2)]
        res_ready = sem("res_ready")
        o_added = sem("o_added")
        x1_stored = [sem(f"x1_stored{n}") for n in range(2)]

        def room(tensor, n):
            flat = tensor[:].rearrange("p a b -> p (a b)")[:, K * D * n:K * D * (n + 1)]
            return flat.rearrange("p (k n) -> p k n", k=K)

        w_raw = {"q": room(probsT, 0), "k": room(probsT, 1), "v": room(probs, 0), "o": room(probsT, 0)}

        SETS = 3 * H
        TILES = T * H
        LN = 12
        BANK = {"q": (1, 1, 1, 1), "k": (0, 0, 1, 0), "v": (1, 0, 1, 0), "o": (0, 0, 1, 0), "x": (1, 0, 1, 0)}

        def proj(kind, n):
            return proj_ps[BANK[kind][n]]

        block = ctx.enter_context(nc.Block())

        def stacked_count(b, g):
            return 64 * (K // 2) * b + 64 * (g // 2 + 1)

        @block.sync
        def _(sp):
            def load_x(b, m):
                if m < 2:
                    wait(sp, x1_stored[m % 2], 32 * (b - 1))
                wait(sp, xt_done, T * b + (m - 1 if m >= 2 else 0))
                stand_alone(sp, sp_turns, b)
                sp.dma_start(x_io[m % 2][:], x[b, P * m:P * m + P]).then_inc(x_loaded[m % 2], 16)

            def load_c(b, k):
                wait(sp, c_low, K * b + k - 1)
                stand_alone(sp, sp_turns, b)
                sp.dma_start(c_in[k % 2][:], ctxT[b, P * k:P * k + P]).then_inc(c_loaded[k % 2], 16)

            def load_mask(b):
                wait(sp, bias_ready, 7 * b)
                stand_alone(sp, sp_turns, b)
                sp.dma_start(mask_row[:].bitcast(I32), mask[b].partition_broadcast(P)).then_inc(mask_loaded, 16)

            def stack(b, g, low_done, stacks, parts, stacked):
                sp.wait_ge(low_done, K * b + g + 1)
                stand_alone(sp, sp_turns, b)
                wait(sp, scores_done, SETS * b + 3 * HG * (g - 1))
                for p in range(PARTS):
                    sp.dma_start(stacks[g % 2][DH * p:DH * p + DH, :, :].bitcast(F32),
                                 staged[parts[p]][:].bitcast(F32)).then_inc(stacked[g % 2], 16)

            def stack_q(b, g):
                stack(b, g, q_low, q_stack, (0, 0, 1, 1), q_stacked)

            def stack_k(b, g):
                stack(b, g, k_low, k_stack, (0, 1, 0, 1), k_stacked)

            def load_residual(b, m, last):
                if m >= 2 or last:
                    sp.wait_ge(x1_stored[m % 2], 32 * b + (16 if m >= 2 else 0))
                else:
                    sp.wait_ge(xt_done, T * (b + 2))
                stand_alone(sp, sp_turns, b)
                sp.dma_start(x_io[m % 2][:], x[b, P * m:P * m + P]).then_inc(res_loaded[m % 2], 16)

            def store_x1(b, m):
                sp.wait_ge(o_added, T * b + m + 1)
                stand_alone(sp, sp_turns, b)
                sp.dma_start(x1[b, P * m:P * m + P], x_io[m % 2][:]).then_inc(x1_stored[m % 2], 16)

            def iteration(i, has_prev, has_next):
                stack_k(i, 1)
                if has_next:
                    load_mask(i + 1)
                if has_prev:
                    load_residual(i - 1, 0, not has_next)
                    load_residual(i - 1, 1, not has_next)
                stack_q(i, 2)
                if has_prev:
                    store_x1(i - 1, 0)
                stack_k(i, 2)
                if has_prev:
                    load_residual(i - 1, 2, False)
                    store_x1(i - 1, 1)
                    load_residual(i - 1, 3, False)
                    store_x1(i - 1, 2)
                    store_x1(i - 1, 3)
                if has_next:
                    load_c(i + 1, 0)
                    load_c(i + 1, 1)
                    load_x(i + 1, 0)
                    load_x(i + 1, 1)
                stack_q(i, 3)
                stack_k(i, 3)
                if has_next:
                    load_x(i + 1, 2)
                    load_c(i + 1, 2)
                    load_x(i + 1, 3)
                    load_c(i + 1, 3)
                    stack_q(i + 1, 0)
                    stack_k(i + 1, 0)
                    stack_q(i + 1, 1)

            for m in range(2):
                load_x(0, m)
            sp.dma_start(w_raw["q"], wqT).then_inc(w_loaded["q"], 16)
            for m in range(2):
                load_c(0, m)
            sp.dma_start(w_raw["k"], wkT).then_inc(w_loaded["k"], 16)
            for n, col in enumerate((bq, bk, bv)):
                sp.dma_start(columns[:, n, :], col).then_inc(small_loaded, 16)
            sp.dma_start(gate[:], g_xattn.partition_broadcast(P)).then_inc(small_loaded, 16)
            sp.dma_start(bo_gated[:], bo.partition_broadcast(P)).then_inc(small_loaded, 16)
            load_mask(0)
            sp.dma_start(w_raw["v"], wvT).then_inc(w_loaded["v"], 16)
            load_x(0, 2)
            load_c(0, 2)
            load_x(0, 3)
            load_c(0, 3)
            sp.wait_ge(w_low, 1)
            sp.dma_start(w_raw["o"], woT).then_inc(w_loaded["o"], 16)
            stack_q(0, 0)
            stack_k(0, 0)
            stack_q(0, 1)
            iteration(0, False, True)
            with sp.Fori(1, B - 1) as i:
                iteration(i, True, True)
            iteration(B - 1, True, False)
            for m in range(2):
                load_residual(B - 1, m, True)
            for m in range(T):
                store_x1(B - 1, m)
                if m < 2:
                    load_residual(B - 1, m + 2, True)
            for n in range(2):
                sp.wait_ge(x1_stored[n], 32 * B)


        @block.gpsimd
        def _(pool):
            def spread_inverse(b, t):
                pool.wait_ge(inv_step, 2 * (K * b + t + 1))
                wait(pool, attn_low, K * b + t)
                stand_alone(pool, pool_turns, b)
                nc.gpsimd.tensor_copy(norm[:].rearrange("p (h d) -> p h d", d=DH),
                                      inverse[:].rearrange("p t h -> p (t h)").unsqueeze(2).broadcast_to([P, T * HG, DH])
                                      ).then_inc(norm_spread, 1)

            def mask_to_bias(b):
                pool.wait_ge(mask_loaded, 16 * (b + 1))
                stand_alone(pool, pool_turns, b)
                nc.gpsimd.tensor_scalar(mask_row[:], mask_row[:].bitcast(I32), 0, MASKED, ALU.is_equal,
                                        ALU.mult).then_inc(mask_ready, 1)

            def add_residual_bias(b, m):
                pool.wait_ge(res_loaded[m % 2], 16 * (T // 2 * b + m // 2 + 1))
                nc.gpsimd.tensor_tensor(x_io[m % 2][:], x_io[m % 2][:], bo_gated[:], ALU.add).then_inc(res_ready, 1)

            def apply_layernorm(b, m):
                pool.wait_ge(ln_stats, T * b + m + 1)
                stand_alone(pool, pool_turns, b)
                nc.gpsimd.tensor_scalar(x_io[m % 2][:], x_io[m % 2][:], moments[:, m % 2, 0:1], rstd[:, m % 2, :],
                                        ALU.subtract, ALU.mult).then_inc(ln_applied, 1)

            def low_part_c(b, k):
                pool.wait_ge(c_high, K * b + k + 1)
                nc.gpsimd.tensor_tensor(cT[1][:, k, :], c_in[k % 2][:], cT[0][:, k, :].bitcast(F32),
                                        ALU.subtract).then_inc(c_low, 1)

            def iteration(i, has_prev, has_next):
                if has_prev:
                    spread_inverse(i - 1, 3)
                if has_next:
                    mask_to_bias(i + 1)
                if has_prev:
                    add_residual_bias(i - 1, 0)
                    add_residual_bias(i - 1, 1)
                spread_inverse(i, 0)
                if has_prev:
                    add_residual_bias(i - 1, 2)
                    add_residual_bias(i - 1, 3)
                if has_next:
                    apply_layernorm(i + 1, 0)
                spread_inverse(i, 1)
                if has_next:
                    apply_layernorm(i + 1, 1)
                    low_part_c(i + 1, 0)
                    apply_layernorm(i + 1, 2)
                    low_part_c(i + 1, 1)
                    apply_layernorm(i + 1, 3)
                    low_part_c(i + 1, 2)
                    low_part_c(i + 1, 3)
                spread_inverse(i, 2)

            nc.gpsimd.memset(ident[:], 0.0).then_inc(pool_const, 1)
            nc.gpsimd.memset(causal[:], 0.0).then_inc(pool_const, 1)
            pool.wait_ge(pool_const, 2)
            nc.gpsimd.affine_select(out=ident[:], in_=ident[:], compare_op=ALU.not_equal, fill=1.0, base=0,
                                    pattern=[[-1, P]], channel_multiplier=1).then_inc(pool_const, 1)
            nc.gpsimd.affine_select(out=causal[:], in_=causal[:], compare_op=ALU.is_ge, fill=MASKED, base=0,
                                    pattern=[[-1, P]], channel_multiplier=1).then_inc(pool_const, 1)
            for m in range(T):
                apply_layernorm(0, m)
                low_part_c(0, m)
            mask_to_bias(0)
            pool.wait_ge(gate_ready, 1)
            nc.gpsimd.tensor_scalar(bo_gated[:], bo_gated[:], gate[:, 0:1], None, ALU.mult).then_inc(pool_const, 1)
            pool.wait_ge(pool_const, 5)
            iteration(0, False, True)
            with pool.Fori(1, B - 1) as i:
                iteration(i, True, True)
            iteration(B - 1, True, False)
            spread_inverse(B - 1, 3)
            for m in range(T):
                add_residual_bias(B - 1, m)

        @block.scalar
        def _(act):
            def high_part_x(b, m):
                act.wait_ge(xt_done, T * b + m + 1)
                wait(act, q_done, K * b)
                nc.scalar.copy(xT[0][:, :, P * m:P * m + P], proj("x", m)[:].rearrange("p (k n) -> p k n", k=K)
                               ).then_inc(xt_high, 1)

            def high_part_c(b, k):
                act.wait_ge(c_loaded[k % 2], 16 * (K // 2 * b + k // 2 + 1))
                wait(act, k_done, K * b)
                nc.scalar.copy(cT[0][:, k, :], c_in[k % 2][:]).then_inc(c_high, 1)

            def high_part_q(b, g):
                act.wait_ge(q_done, K * b + g + 1)
                if g > 0:
                    act.wait_ge(k_stacked[(g - 1) % 2], stacked_count(b, g - 1))
                else:
                    wait(act, k_stacked[1], 64 * (K // 2) * b)
                nc.scalar.activation(staged[0][:], proj("q", g)[:], ACT.Identity, bias=columns[:, 0, g:g + 1]
                                     ).then_inc(q_high, 1)

            def high_part_k(b, g):
                act.wait_ge(k_done, K * b + g + 1)
                act.wait_ge(q_stacked[g % 2], stacked_count(b, g))
                nc.scalar.activation(staged[0][:], proj("k", g)[:], ACT.Identity, bias=columns[:, 1, g:g + 1]
                                     ).then_inc(k_high, 1)

            def copy_v(b, m):
                act.wait_ge(v_done, T * b + m + 1)
                wait(act, values_done, K * b)
                nc.scalar.copy(v[:, m, :], proj("v", m)[:]).then_inc(v_copied, 1)

            def copy_norm(b, t):
                act.wait_ge(norm_done, K * b + t + 1)
                nc.scalar.copy(norm[:], norm_ps[:]).then_inc(norm_copied, 1)

            def high_part_attn(b, t):
                act.wait_ge(normalised, K * b + t + 1)
                wait(act, o_done, T * b)
                nc.scalar.activation(attn[0][:, t, :], norm[:], ACT.Identity, bias=columns[:, 2, t:t + 1]
                                     ).then_inc(attn_high, 1)

            def transposed(b, h, n):
                act.wait_ge(pt_done, SETS * b + 3 * h + n + 1)
                wait(act, values_done, K * b + h // HG)
                lo, hi = PT_COLS[n]
                nc.scalar.copy(probsT[:, h % HG, lo:hi], pt_ps[n % 2][:, 0:hi - lo]).then_inc(pt_act, 1)

            def exponent(b, h, t):
                act.wait_ge(scores_read, TILES * b + T * h + t + 1)
                here = probs[:, h % 2, SEG[t]:SEG[t + 1]]
                at = (h // HG, t, h % HG)
                nc.scalar.activation(here, here, ACT.Exp, bias=least[:, at[0], at[1], at[2]:at[2] + 1], scale=-1.0,
                                     accum_out=sums[:, at[0], at[1], at[2]:at[2] + 1]).then_inc(exp_done, 1)

            def iteration(i, has_prev, has_next):
                for s in range(H):
                    before = (i, s - 1) if s > 0 else (i - 1, H - 1)
                    if s > 0 or has_prev:
                        transposed(*before, 0)
                    exponent(i, s, 0)
                    exponent(i, s, 1)
                    exponent(i, s, 2)
                    if s > 0 or has_prev:
                        transposed(*before, 2)
                    exponent(i, s, 3)
                    if s == 0:
                        high_part_k(i, 1)
                        if has_prev:
                            copy_norm(i - 1, 3)
                    if s == 1:
                        copy_v(i, 0)
                        copy_v(i, 1)
                        if has_prev:
                            high_part_attn(i - 1, 3)
                    if s == 2:
                        copy_v(i, 2)
                        copy_v(i, 3)
                    if s == 3:
                        high_part_q(i, 2)
                    if s == 4:
                        high_part_k(i, 2)
                        copy_norm(i, 0)
                    if s == 7:
                        high_part_q(i, 3)
                        high_part_attn(i, 0)
                    if s == 8:
                        high_part_k(i, 3)
                        if has_next:
                            high_part_x(i + 1, 0)
                            high_part_c(i + 1, 0)
                        copy_norm(i, 1)
                    if s == 9:
                        if has_next:
                            high_part_x(i + 1, 1)
                            high_part_c(i + 1, 1)
                        high_part_attn(i, 1)
                    if s == 10 and has_next:
                        high_part_c(i + 1, 2)
                    if s == 11 and has_next:
                        high_part_x(i + 1, 2)
                        high_part_c(i + 1, 3)
                    if s == 12:
                        if has_next:
                            high_part_x(i + 1, 3)
                            high_part_q(i + 1, 0)
                        copy_norm(i, 2)
                    if s == 13:
                        if has_next:
                            high_part_k(i + 1, 0)
                        high_part_attn(i, 2)
                    if s == 15 and has_next:
                        high_part_q(i + 1, 1)

            def split_weights(n, name):
                act.wait_ge(w_loaded[name], 16)
                nc.scalar.copy(w[name][0][:], w_raw[name]).then_inc(w_high, 1)

            for m in range(2):
                high_part_x(0, m)
                high_part_c(0, m)
            split_weights(0, "q")
            split_weights(1, "k")
            for m in range(2, T):
                high_part_x(0, m)
                high_part_c(0, m)
            act.wait_ge(small_loaded, 16 * 5)
            high_part_q(0, 0)
            high_part_k(0, 0)
            split_weights(2, "v")
            high_part_q(0, 1)
            nc.scalar.activation(gate[:], gate[:], ACT.Tanh).then_inc(gate_ready, 1)
            split_weights(3, "o")
            iteration(0, False, True)
            with act.Fori(1, B - 1) as i:
                iteration(i, True, True)
            iteration(B - 1, True, False)
            for n in (0, 2):
                transposed(B - 1, H - 1, n)
            copy_norm(B - 1, 3)
            high_part_attn(B - 1, 3)

        @block.vector
        def _(dve):
            def layernorm_stats(b, m):
                at = LN * (T * b + m)
                wait(dve, ln_stats, T * b + m)
                dve.wait_ge(x_loaded[m % 2], 16 * (T // 2 * b + m // 2 + 1))
                nc.vector.bn_stats(stats[:], x_io[m % 2][:]).then_inc(ln_step, 1)
                dve.wait_ge(ln_step, at + 1)
                wait(dve, ln_applied, T * b + m - 1)
                stand_alone(dve, dve_turns, b)
                nc.vector.bn_aggr(moments[:, m % 2, :], stats[:]).then_inc(ln_step, 1)
                dve.wait_ge(ln_step, at + 2)
                variance = newton[:, 0:1]
                guess, power = newton[:, 1:2], newton[:, 2:3]
                nc.vector.tensor_scalar(variance, moments[:, m % 2, 1:2], LN_EPS, None, ALU.add).then_inc(ln_step, 1)
                dve.wait_ge(ln_step, at + 3)
                nc.vector.tensor_scalar(guess.bitcast(I32), variance.bitcast(I32), -0.5, RSQRT_SEED, ALU.mult,
                                        ALU.add).then_inc(ln_step, 1)
                dve.wait_ge(ln_step, at + 4)
                for n in range(3):
                    nc.vector.scalar_tensor_tensor(out=power, in0=guess, scalar=variance, in1=guess, op0=ALU.mult,
                                                   op1=ALU.mult).then_inc(ln_step, 1)
                    dve.wait_ge(ln_step, at + 5 + 3 * n)
                    nc.vector.tensor_scalar(power, power, -0.5, 1.5, ALU.mult, ALU.add).then_inc(ln_step, 1)
                    dve.wait_ge(ln_step, at + 6 + 3 * n)
                    if n < 2:
                        nc.vector.tensor_tensor(guess, guess, power, ALU.mult).then_inc(ln_step, 1)
                        dve.wait_ge(ln_step, at + 7 + 3 * n)
                nc.vector.tensor_tensor(rstd[:, m % 2, :], guess, power, ALU.mult).then_inc(ln_stats, 1)

            def low_part_x(b, m):
                dve.wait_ge(xt_high, T * b + m + 1)
                nc.vector.tensor_tensor(xT[1][:, :, P * m:P * m + P], proj("x", m)[:].rearrange("p (k n) -> p k n", k=K),
                                        xT[0][:, :, P * m:P * m + P].bitcast(F32), ALU.subtract).then_inc(xt_low, 1)

            def low_part_q(b, g):
                dve.wait_ge(q_high, K * b + g + 1)
                nc.vector.scalar_tensor_tensor(out=staged[1][:], in0=proj("q", g)[:], scalar=columns[:, 0, g:g + 1],
                                               in1=staged[0][:].bitcast(F32), op0=ALU.add, op1=ALU.subtract
                                               ).then_inc(q_low, 1)

            def low_part_k(b, g):
                dve.wait_ge(k_high, K * b + g + 1)
                nc.vector.scalar_tensor_tensor(out=staged[1][:], in0=proj("k", g)[:], scalar=columns[:, 1, g:g + 1],
                                               in1=staged[0][:].bitcast(F32), op0=ALU.add, op1=ALU.subtract
                                               ).then_inc(k_low, 1)

            def build_bias(b):
                dve.wait_ge(mask_ready, b + 1)
                wait(dve, scores_read, TILES * b)
                for t in range(T):
                    nc.vector.tensor_tensor(bias[:, SEG[t + 1] - P:SEG[t + 1]], mask_row[:, P * t:P * t + P], causal[:],
                                            ALU.add).then_inc(bias_ready, 1)
                    if t > 0:
                        nc.vector.tensor_copy(bias[:, SEG[t]:SEG[t + 1] - P], mask_row[:, 0:P * t]).then_inc(bias_ready, 1)
                dve.wait_ge(bias_ready, 7 * (b + 1))

            def bias_scores(b, h, t):
                c = max(t - 1, 0)
                if t != 1:
                    dve.wait_ge(scores_done, SETS * b + 3 * h + c + 1)
                    if t == 0:
                        wait(dve, pt_done, SETS * b + 3 * (h - 1))
                    stand_alone(dve, dve_turns, b)
                at = P if t == 1 else 0
                width = P * (t + 1)
                nc.vector.tensor_tensor_reduce(
                    out=probs[:, h % 2, SEG[t]:SEG[t + 1]], in0=score_ps[(h + c) % 2][:, at:at + width],
                    in1=bias[:, SEG[t]:SEG[t + 1]], scale=-SCALE, scalar=3e38, op0=ALU.add, op1=ALU.min,
                    accum_out=least[:, h // HG, t, h % HG:h % HG + 1]).then_inc(scores_read, 1)

            def transposed(b, h):
                dve.wait_ge(pt_done, SETS * b + 3 * h + 2)
                wait(dve, values_done, K * b + h // HG)
                lo, hi = PT_COLS[1]
                nc.vector.tensor_copy(probsT[:, h % HG, lo:hi], pt_ps[1][:, 0:hi - lo]).then_inc(pt_dve, 1)

            def invert_sums(b, t):
                dve.wait_ge(exp_done, TILES * b + T * HG * (t + 1))
                nc.vector.scalar_tensor_tensor(out=live[:], in0=least[:, t], scalar=-MASKED / 100, in1=sums[:, t],
                                               op0=ALU.is_lt, op1=ALU.mult).then_inc(inv_step, 1)
                dve.wait_ge(inv_step, 2 * (K * b + t) + 1)
                wait(dve, norm_spread, K * b + t)
                nc.vector.reciprocal(inverse[:], live[:]).then_inc(inv_step, 1)

            def normalise(b, t):
                dve.wait_ge(norm_copied, K * b + t + 1)
                dve.wait_ge(values_done, K * b + t + 1)
                nc.vector.tensor_tensor(norm[:], value_ps[:], norm[:], ALU.mult).then_inc(normalised, 1)

            def low_part_attn(b, t):
                dve.wait_ge(attn_high, K * b + t + 1)
                nc.vector.scalar_tensor_tensor(out=attn[1][:, t, :], in0=norm[:], scalar=columns[:, 2, t:t + 1],
                                               in1=attn[0][:, t, :].bitcast(F32), op0=ALU.add, op1=ALU.subtract
                                               ).then_inc(attn_low, 1)

            def add_output(b, m):
                dve.wait_ge(o_done, T * b + m + 1)
                dve.wait_ge(res_ready, T * b + m + 1)
                nc.vector.scalar_tensor_tensor(out=x_io[m % 2][:], in0=proj("o", m)[:], scalar=gate[:, 0:1],
                                               in1=x_io[m % 2][:], op0=ALU.mult, op1=ALU.add).then_inc(o_added, 1)

            def iteration(i, has_prev, has_next):
                build_bias(i)
                for s in range(H):
                    for t in range(3):
                        bias_scores(i, s, t)
                    if s > 0:
                        transposed(i, s - 1)
                    elif has_prev:
                        transposed(i - 1, H - 1)
                    bias_scores(i, s, 3)
                    if s == 0:
                        if has_prev:
                            invert_sums(i - 1, 3)
                        low_part_k(i, 1)
                    if s == 1 and has_prev:
                        normalise(i - 1, 3)
                    if s == 2 and has_prev:
                        low_part_attn(i - 1, 3)
                    if s == 3:
                        low_part_q(i, 2)
                        if has_prev:
                            add_output(i - 1, 0)
                    if s == 4:
                        invert_sums(i, 0)
                        low_part_k(i, 2)
                        if has_prev:
                            add_output(i - 1, 1)
                    if s == 5 and has_prev:
                        add_output(i - 1, 2)
                    if s == 6 and has_prev:
                        add_output(i - 1, 3)
                    if s == 7:
                        normalise(i, 0)
                        low_part_q(i, 3)
                        if has_next:
                            layernorm_stats(i + 1, 0)
                    if s == 8:
                        low_part_attn(i, 0)
                        invert_sums(i, 1)
                        low_part_k(i, 3)
                        if has_next:
                            low_part_x(i + 1, 0)
                            layernorm_stats(i + 1, 1)
                    if s == 9:
                        normalise(i, 1)
                        if has_next:
                            low_part_x(i + 1, 1)
                    if s == 10:
                        low_part_attn(i, 1)
                        if has_next:
                            layernorm_stats(i + 1, 2)
                    if s == 11 and has_next:
                        low_part_x(i + 1, 2)
                        layernorm_stats(i + 1, 3)
                    if s == 12:
                        invert_sums(i, 2)
                        if has_next:
                            low_part_x(i + 1, 3)
                            low_part_q(i + 1, 0)
                    if s == 13:
                        normalise(i, 2)
                        if has_next:
                            low_part_k(i + 1, 0)
                    if s == 14:
                        low_part_attn(i, 2)
                    if s == 15 and has_next:
                        low_part_q(i + 1, 1)

            def split_weights(n, name):
                dve.wait_ge(w_high, n + 1)
                nc.vector.tensor_tensor(w[name][1][:], w_raw[name], w[name][0][:].bitcast(F32),
                                        ALU.subtract).then_inc(w_low, 1)

            layernorm_stats(0, 0)
            layernorm_stats(0, 1)
            low_part_x(0, 0)
            low_part_x(0, 1)
            split_weights(0, "q")
            split_weights(1, "k")
            layernorm_stats(0, 2)
            low_part_x(0, 2)
            layernorm_stats(0, 3)
            low_part_x(0, 3)
            low_part_q(0, 0)
            low_part_k(0, 0)
            split_weights(2, "v")
            low_part_q(0, 1)
            split_weights(3, "o")
            dve.wait_ge(w_low, 4)
            dve.wait_ge(pool_const, 5)
            iteration(0, False, True)
            with dve.Fori(1, B - 1) as i:
                iteration(i, True, True)
            iteration(B - 1, True, False)
            transposed(B - 1, H - 1)
            invert_sums(B - 1, 3)
            normalise(B - 1, 3)
            low_part_attn(B - 1, 3)
            for m in range(T):
                add_output(B - 1, m)

        @block.tensor
        def _(pe):
            def scores(b, h, c):
                g, j = h // HG, h % HG
                if j == 0 and c == 0:
                    pe.wait_ge(q_stacked[g % 2], stacked_count(b, g))
                    pe.wait_ge(k_stacked[g % 2], stacked_count(b, g))
                wait(pe, scores_read, TILES * b + T * h + (-1, 0, 2)[c])
                bank = score_ps[(h + c) % 2]
                for t in ((0, 1), (2,), (3,))[c]:
                    at = P if t == 1 else 0
                    last = nc.tensor.matmul(bank[:, at:at + P * (t + 1)], q_stack[g % 2][:, j, P * t:P * t + P],
                                            k_stack[g % 2][:, j, 0:P * (t + 1)], start=True, stop=True)
                last.then_inc(scores_done, 1)

            def transpose_probs(b, h, n):
                if n == 0:
                    pe.wait_ge(exp_done, TILES * b + T * (h + 1))
                if n == 1:
                    wait(pe, pt_dve, H * b + h)
                else:
                    wait(pe, pt_act, 2 * (H * b + h) + n // 2)
                for k in PT_SETS[n]:
                    for t in range(k, T):
                        at = PT_AT[k] - PT_COLS[n][0] + P * (t - k)
                        last = nc.tensor.transpose(pt_ps[n % 2][:, at:at + P],
                                                   probs[:, h % 2, SEG[t] + P * k:SEG[t] + P * k + P], ident[:])
                last.then_inc(pt_done, 1)

            def transpose_inverse(b, t):
                pe.wait_ge(norm_spread, K * b + t + 1)
                wait(pe, norm_copied, K * b + t)
                for n in range(T):
                    last = nc.tensor.transpose(norm_ps[:, P * n:P * n + P], norm[:, P * n:P * n + P], ident[:])
                last.then_inc(norm_done, 1)

            def values(b, t):
                pe.wait_ge(pt_act, 2 * H * b + 2 * HG * (t + 1))
                pe.wait_ge(pt_dve, H * b + HG * (t + 1))
                if t == 0:
                    pe.wait_ge(v_copied, T * (b + 1))
                wait(pe, normalised, K * b + t)
                for k in range(T):
                    for j in range(HG):
                        last = nc.tensor.matmul(value_ps[DH * j:DH * j + DH, P * k:S],
                                                v[:, k, P * t + DH * j:P * t + DH * j + DH],
                                                probsT[:, j, PT_AT[k]:PT_AT[k] + S - P * k],
                                                start=(k == 0), stop=(k == T - 1), skip_group_check=True)
                last.then_inc(values_done, 1)

            def project_q(b, g, has_prev=False):
                if g == 0:
                    pe.wait_ge(xt_low, T * (b + 1))
                    pe.wait_ge(xt_low, T * b + 3)
                elif g == 1:
                    pe.wait_ge(q_low, K * b + 1)
                elif g == 2:
                    pe.wait_ge(v_copied, T * b + 3)
                elif has_prev:
                    pe.wait_ge(o_added, T * b - 1)
                else:
                    pe.wait_ge(k_low, K * b + 3)
                exact_product(nc, proj("q", g)[:], lambda k: [part[:, k, P * g:P * g + P] for part in w["q"]],
                              lambda k: [part[:, k, :] for part in xT], K).then_inc(q_done, 1)

            def project_k(b, g, has_prev=False):
                if g == 0:
                    pe.wait_ge(c_low, K * (b + 1))
                    pe.wait_ge(xt_low, T * (b + 1))
                elif g == 1:
                    pe.wait_ge(k_low, K * b + 1)
                elif g == 2:
                    pe.wait_ge(q_low, K * b + 3)
                elif has_prev:
                    pe.wait_ge(o_added, T * b)
                else:
                    pe.wait_ge(v_copied, T * (b + 1))
                exact_product(nc, proj("k", g)[:], lambda k: [part[:, k, P * g:P * g + P] for part in w["k"]],
                              lambda k: [part[:, k, :] for part in cT], K).then_inc(k_done, 1)

            def project_v(b, m):
                if m == 0:
                    pe.wait_ge(q_low, K * b + 2)
                elif m == 1:
                    pe.wait_ge(k_low, K * b + 2)
                else:
                    pe.wait_ge(v_copied, T * b + m - 1)
                exact_product(nc, proj("v", m)[:], lambda k: [part[:, k, P * m:P * m + P] for part in cT],
                              lambda k: [part[:, k, :] for part in w["v"]], K).then_inc(v_done, 1)

            def project_o(b, m, last=False):
                if m == 0:
                    pe.wait_ge(attn_low, K * (b + 1))
                    pe.wait_ge(k_low, K * (b + 1)) if last else pe.wait_ge(v_copied, T * (b + 2))
                elif m == 2:
                    pe.wait_ge(q_low, K * (b + 1)) if last else pe.wait_ge(k_low, K * (b + 1) + 3)
                else:
                    pe.wait_ge(o_added, T * b + (1 if m == 1 else 2))
                exact_product(nc, proj("o", m)[:], lambda k: [part[:, k, P * m:P * m + P] for part in attn],
                              lambda k: [part[:, k, :] for part in w["o"]], K).then_inc(o_done, 1)

            def transpose_x(b, m):
                pe.wait_ge(ln_applied, T * b + m + 1)
                if m == 0:
                    wait(pe, q_low, K * b)
                elif m == 1:
                    wait(pe, k_low, K * b)
                else:
                    pe.wait_ge(xt_low, T * b + m - 1)
                for k in range(K):
                    last = nc.tensor.transpose(proj("x", m)[:, P * k:P * k + P], x_io[m % 2][:, P * k:P * k + P], ident[:])
                last.then_inc(xt_done, 1)

            def iteration(i, has_prev, has_next):
                for s in range(H):
                    before = (i, s - 1) if s > 0 else (i - 1, H - 1)
                    scores(i, s, 0)
                    scores(i, s, 1)
                    if s > 0 or has_prev:
                        transpose_probs(*before, 0)
                    scores(i, s, 2)
                    if s > 0 or has_prev:
                        transpose_probs(*before, 1)
                        transpose_probs(*before, 2)
                    if s == 0:
                        project_k(i, 1)
                        if has_prev:
                            transpose_inverse(i - 1, 3)
                            values(i - 1, 3)
                    if s == 1:
                        project_v(i, 0)
                        project_v(i, 1)
                    if s == 2:
                        project_v(i, 2)
                        project_v(i, 3)
                    if s == 3:
                        project_q(i, 2)
                        if has_prev:
                            project_o(i - 1, 0)
                    if s == 4:
                        project_k(i, 2)
                        if has_prev:
                            project_o(i - 1, 1)
                        transpose_inverse(i, 0)
                        values(i, 0)
                    if s == 5 and has_prev:
                        project_o(i - 1, 2)
                    if s == 6 and has_prev:
                        project_o(i - 1, 3)
                    if s == 7:
                        project_q(i, 3, has_prev)
                    if s == 8:
                        project_k(i, 3, has_prev)
                        if has_next:
                            transpose_x(i + 1, 0)
                        transpose_inverse(i, 1)
                        values(i, 1)
                    if s == 9 and has_next:
                        transpose_x(i + 1, 1)
                    if s == 11 and has_next:
                        transpose_x(i + 1, 2)
                    if s == 12:
                        if has_next:
                            transpose_x(i + 1, 3)
                            project_q(i + 1, 0)
                        transpose_inverse(i, 2)
                        values(i, 2)
                    if s == 13 and has_next:
                        project_k(i + 1, 0)
                    if s == 15 and has_next:
                        project_q(i + 1, 1)

            pe.wait_ge(pool_const, 4)
            for m in range(T):
                transpose_x(0, m)
            pe.wait_ge(w_low, 1)
            project_q(0, 0)
            pe.wait_ge(w_low, 2)
            project_k(0, 0)
            project_q(0, 1)
            pe.wait_ge(w_low, 3)
            iteration(0, False, True)
            with pe.Fori(1, B - 1) as i:
                iteration(i, True, True)
            iteration(B - 1, True, False)
            for n in range(3):
                transpose_probs(B - 1, H - 1, n)
            transpose_inverse(B - 1, 3)
            values(B - 1, 3)
            for m in range(T):
                project_o(B - 1, m, True)


def channel_mix_phase(nc, x1, g_ffn, wrT, wkT, wvT, mu_r, mu_k, out):
    B, S, D = x1.shape
    T = S // P
    K = D // P

    with ExitStack() as ctx:
        def sb(name, shape, dt=F32):
            return ctx.enter_context(nc.sbuf_tensor(name, shape, dt))

        def psums(name, n):
            return [ctx.enter_context(nc.psum_tensor(f"{name}{i}", [P, 512], F32)) for i in range(n)]

        def sem(name):
            return ctx.enter_context(nc.semaphore(name))

        def pair(name):
            return [sb(f"{name}_{part}", [P, K, S], F32R) for part in ("high", "low")]

        w = {n: pair(f"ffn_w{n}") for n in "krv"}
        w_raw = {"k": sb("ffn_raw_k", [P, K, D]), "r": sb("ffn_raw_r", [P, K, D])}
        w_raw["v"] = w_raw["k"]
        x_in = sb("ffn_x_in", [P, T, D])
        xT = sb("ffn_xT", [P, K, S + 1])
        delta = sb("delta", [P, K, S])
        mixed = {n: sb(f"mixed_{n}", [P, 2, S]) for n in "kr"}
        mix = {n: pair(f"mix_{n}") for n in "kr"}
        relu = sb("relu", [P, 2, S])
        square = sb("square", [P, 2, S])
        kact = pair("kact")
        r_tanh = sb("r_tanh", [P, T, D])
        y = sb("y", [P, 2, D])
        res = sb("res", [P, T, D])
        ident = sb("ffn_ident", [P, P])
        mu = sb("mu", [P, 2, K])
        gate = sb("ffn_gate", [P, 2])
        stats = sb("ffn_stats", [P, T, 6])
        moments = sb("ffn_moments", [P, T, 2])
        rstd = sb("ffn_rstd", [P, T])
        newton = sb("ffn_newton", [P, 3, T])

        x_ps, k_ps, r_ps, v_ps = psums("ffn_x_ps", 2), psums("ffn_k_ps", 2), psums("ffn_r_ps", 2), psums("ffn_v_ps", 2)

        w_loaded = {n: sem(f"ffn_w{n}_loaded") for n in "krv"}
        sp_turns, pool_turns, dve_turns = sem("ffn_sp_turns"), sem("ffn_pool_turns"), sem("ffn_dve_turns")
        w_high, w_low = sem("ffn_w_high"), sem("ffn_w_low")
        small_loaded, gate_ready, pool_const = sem("ffn_small"), sem("ffn_gate_ready"), sem("ffn_pool_const")
        zeroed = sem("zeroed")
        x_loaded = sem("ffn_x_loaded")
        ln_step = sem("ffn_ln_step")
        ln_stats = sem("ffn_ln_stats")
        ln_applied = sem("ffn_ln_applied")
        xt_done = sem("ffn_xt_done")
        xt_copied = sem("ffn_xt_copied")
        delta_done = sem("delta_done")
        mixed_done = {n: sem(f"mixed_{n}_done") for n in "kr"}
        mix_high = {n: sem(f"mix_{n}_high") for n in "kr"}
        mix_low = {n: sem(f"mix_{n}_low") for n in "kr"}
        k_done, r_done, v_done = sem("ffn_k_done"), sem("ffn_r_done"), sem("ffn_v_done")
        relu_done, square_done = sem("relu_done"), sem("square_done")
        kact_high, kact_low = sem("kact_high"), sem("kact_low")
        r_ready = sem("r_ready")
        y_done, added = sem("y_done"), sem("added")
        res_loaded = [sem(f"ffn_res_loaded{m}") for m in range(T)]
        stored = [sem(f"ffn_stored{m}") for m in range(T)]

        LN = T + T + 10
        block = ctx.enter_context(nc.Block())

        @block.sync
        def _(sp):
            def load_x(b):
                wait(sp, xt_done, T * b)
                stand_alone(sp, sp_turns, b)
                sp.dma_start(x_in[:], x1[b].rearrange("(t p) d -> p t d", p=P)).then_inc(x_loaded, 16)

            def load_res(b, m):
                wait(sp, stored[m], 16 * b)
                stand_alone(sp, sp_turns, b)
                sp.dma_start(res[:, m, :], x1[b, P * m:P * m + P]).then_inc(res_loaded[m], 16)

            def store(b, m):
                sp.wait_ge(added, T * b + m + 1)
                stand_alone(sp, sp_turns, b)
                sp.dma_start(out[b, P * m:P * m + P], res[:, m, :]).then_inc(stored[m], 16)

            def iteration(i, has_next):
                for m in range(T):
                    load_res(i, m)
                if has_next:
                    load_x(i + 1)
                for m in range(T):
                    store(i, m)

            load_x(0)
            sp.dma_start(w_raw["k"][:], wkT).then_inc(w_loaded["k"], 16)
            sp.dma_start(w_raw["r"][:], wrT).then_inc(w_loaded["r"], 16)
            sp.dma_start(mu[:, 0, :], mu_k).then_inc(small_loaded, 16)
            sp.dma_start(mu[:, 1, :], mu_r).then_inc(small_loaded, 16)
            sp.dma_start(gate[:, 0:1], g_ffn.partition_broadcast(P)).then_inc(small_loaded, 16)
            sp.wait_ge(w_low, 1)
            sp.dma_start(w_raw["v"][:], wvT).then_inc(w_loaded["v"], 16)
            iteration(0, True)
            with sp.Fori(1, B - 1) as i:
                iteration(i, True)
            iteration(B - 1, False)
            for m in range(T):
                sp.wait_ge(stored[m], 16 * B)

        @block.gpsimd
        def _(pool):
            def apply_layernorm(b, m):
                pool.wait_ge(ln_stats, b + 1)
                stand_alone(pool, pool_turns, b)
                nc.gpsimd.tensor_scalar(x_in[:, m, :], x_in[:, m, :], moments[:, m, 0:1], rstd[:, m:m + 1],
                                        ALU.subtract, ALU.mult).then_inc(ln_applied, 1)

            def take_delta(b, k):
                pool.wait_ge(xt_copied, T * (b + 1))
                nc.gpsimd.tensor_tensor(delta[:, k, :], xT[:, k, 1:S + 1], xT[:, k, 0:S], ALU.subtract).then_inc(delta_done, 1)

            def low_part_act(b, k):
                pool.wait_ge(kact_high, K * b + k + 1)
                nc.gpsimd.tensor_tensor(kact[1][:, k, :], square[:, k % 2, :], kact[0][:, k, :].bitcast(F32),
                                        ALU.subtract).then_inc(kact_low, 1)

            def iteration(i, has_next):
                if has_next:
                    apply_layernorm(i + 1, 0)
                low_part_act(i, 0)
                if has_next:
                    apply_layernorm(i + 1, 1)
                low_part_act(i, 1)
                if has_next:
                    apply_layernorm(i + 1, 2)
                low_part_act(i, 2)
                if has_next:
                    apply_layernorm(i + 1, 3)
                low_part_act(i, 3)
                if has_next:
                    for k in range(K):
                        take_delta(i + 1, k)

            nc.gpsimd.memset(ident[:], 0.0).then_inc(pool_const, 1)
            pool.wait_ge(pool_const, 1)
            nc.gpsimd.affine_select(out=ident[:], in_=ident[:], compare_op=ALU.not_equal, fill=1.0, base=0,
                                    pattern=[[-1, P]], channel_multiplier=1).then_inc(pool_const, 1)
            for m in range(T):
                apply_layernorm(0, m)
            pool.wait_ge(zeroed, 1)
            for k in range(K):
                take_delta(0, k)
            iteration(0, True)
            with pool.Fori(1, B - 1) as i:
                iteration(i, True)
            iteration(B - 1, False)

        @block.scalar
        def _(act):
            def copy_x(b, m):
                act.wait_ge(xt_done, T * b + m + 1)
                wait(act, mixed_done["r"], K * b)
                nc.scalar.copy(xT[:, :, 1 + P * m:1 + P * m + P], x_ps[m % 2][:].rearrange("p (k n) -> p k n", k=K)
                               ).then_inc(xt_copied, 1)

            def high_part_mix(b, n, k, done):
                act.wait_ge(mixed_done[n], K * b + k + 1)
                wait(act, done, K * b)
                nc.scalar.copy(mix[n][0][:, k, :], mixed[n][:, k % 2, :]).then_inc(mix_high[n], 1)

            def relu_k(b, k):
                act.wait_ge(k_done, K * b + k + 1)
                wait(act, square_done, K * b + k - 1)
                nc.scalar.activation(relu[:, k % 2, :], k_ps[k % 2][:], ACT.Relu).then_inc(relu_done, 1)

            def high_part_act(b, k):
                act.wait_ge(square_done, K * b + k + 1)
                wait(act, v_done, T * b)
                nc.scalar.copy(kact[0][:, k, :], square[:, k % 2, :]).then_inc(kact_high, 1)

            def gate_r(b, m):
                act.wait_ge(r_done, T * b + m + 1)
                wait(act, y_done, T * (b - 1) + m + 1)
                nc.scalar.activation(r_tanh[:, m, :], r_ps[m % 2][:], ACT.Tanh, scale=0.5).then_inc(r_ready, 1)

            def iteration(i, has_next):
                relu_k(i, 0)
                for k in range(1, K):
                    relu_k(i, k)
                    high_part_act(i, k - 1)
                high_part_act(i, K - 1)
                for m in range(T):
                    if has_next:
                        copy_x(i + 1, m)
                for m in range(T):
                    gate_r(i, m)
                    if has_next:
                        high_part_mix(i + 1, "k", m, k_done)
                if has_next:
                    for k in range(K):
                        high_part_mix(i + 1, "r", k, r_done)

            for m in range(T):
                copy_x(0, m)
            for n, name in enumerate("krv"):
                act.wait_ge(w_loaded[name], 16)
                nc.scalar.copy(w[name][0][:], w_raw[name][:]).then_inc(w_high, 1)
            for n, done in (("k", k_done), ("r", r_done)):
                for k in range(K):
                    high_part_mix(0, n, k, done)
            act.wait_ge(small_loaded, 16 * 3)
            nc.scalar.activation(gate[:, 1:2], gate[:, 0:1], ACT.Tanh).then_inc(gate_ready, 1)
            iteration(0, True)
            with act.Fori(1, B - 1) as i:
                iteration(i, True)
            iteration(B - 1, False)

        @block.vector
        def _(dve):
            def layernorm_stats(b):
                at = LN * b
                dve.wait_ge(x_loaded, 16 * (b + 1))
                wait(dve, ln_applied, T * b)
                wait(dve, ln_stats, b)
                for m in range(T):
                    nc.vector.bn_stats(stats[:, m, :], x_in[:, m, :]).then_inc(ln_step, 1)
                dve.wait_ge(ln_step, at + T)
                stand_alone(dve, dve_turns, b)
                for m in range(T):
                    nc.vector.bn_aggr(moments[:, m, :], stats[:, m, :]).then_inc(ln_step, 1)
                dve.wait_ge(ln_step, at + 2 * T)
                variance, guess, power = newton[:, 0, :], newton[:, 1, :], newton[:, 2, :]
                at += 2 * T
                nc.vector.tensor_scalar(variance, moments[:, :, 1], LN_EPS, None, ALU.add).then_inc(ln_step, 1)
                dve.wait_ge(ln_step, at + 1)
                nc.vector.tensor_scalar(guess.bitcast(I32), variance.bitcast(I32), -0.5, RSQRT_SEED, ALU.mult,
                                        ALU.add).then_inc(ln_step, 1)
                dve.wait_ge(ln_step, at + 2)
                for n in range(3):
                    nc.vector.tensor_tensor(power, guess, guess, ALU.mult).then_inc(ln_step, 1)
                    dve.wait_ge(ln_step, at + 3 + 3 * n)
                    nc.vector.scalar_tensor_tensor(out=power, in0=power, scalar=-0.5, in1=variance, op0=ALU.mult,
                                                   op1=ALU.mult).then_inc(ln_step, 1)
                    dve.wait_ge(ln_step, at + 4 + 3 * n)
                    step = nc.vector.scalar_tensor_tensor(out=rstd[:] if n == 2 else guess, in0=power, scalar=1.5,
                                                          in1=guess, op0=ALU.add, op1=ALU.mult)
                    if n < 2:
                        step.then_inc(ln_step, 1)
                        dve.wait_ge(ln_step, at + 5 + 3 * n)
                    else:
                        step.then_inc(ln_stats, 1)

            def mix_tokens(b, n, k):
                dve.wait_ge(delta_done, K * b + k + 1)
                wait(dve, mix_low[n], K * b + k - 1)
                col = "kr".index(n)
                nc.vector.scalar_tensor_tensor(out=mixed[n][:, k % 2, :], in0=delta[:, k, :], scalar=mu[:, col, k:k + 1],
                                               in1=xT[:, k, 0:S], op0=ALU.mult, op1=ALU.add).then_inc(mixed_done[n], 1)

            def low_part_mix(b, n, k):
                dve.wait_ge(mix_high[n], K * b + k + 1)
                nc.vector.tensor_tensor(mix[n][1][:, k, :], mixed[n][:, k % 2, :], mix[n][0][:, k, :].bitcast(F32),
                                        ALU.subtract).then_inc(mix_low[n], 1)

            def square_k(b, k):
                dve.wait_ge(relu_done, K * b + k + 1)
                wait(dve, kact_low, K * b + k - 1)
                nc.vector.scalar_tensor_tensor(out=square[:, k % 2, :], in0=k_ps[k % 2][:], scalar=0.0,
                                               in1=relu[:, k % 2, :], op0=ALU.max, op1=ALU.mult).then_inc(square_done, 1)

            def combine(b, m):
                dve.wait_ge(v_done, T * b + m + 1)
                dve.wait_ge(r_ready, T * b + m + 1)
                wait(dve, added, T * b + m - 1)
                nc.vector.scalar_tensor_tensor(out=y[:, m % 2, :], in0=r_tanh[:, m, :], scalar=1.0, in1=v_ps[m % 2][:],
                                               op0=ALU.add, op1=ALU.mult).then_inc(y_done, 1)
                dve.wait_ge(y_done, T * b + m + 1)
                dve.wait_ge(res_loaded[m], 16 * (b + 1))
                nc.vector.scalar_tensor_tensor(out=res[:, m, :], in0=y[:, m % 2, :], scalar=gate[:, 0:1], in1=res[:, m, :],
                                               op0=ALU.mult, op1=ALU.add).then_inc(added, 1)

            def iteration(i, has_next):
                if has_next:
                    layernorm_stats(i + 1)
                for k in range(K):
                    square_k(i, k)
                if has_next:
                    mix_tokens(i + 1, "k", 0)
                    for k in range(1, K):
                        mix_tokens(i + 1, "k", k)
                        low_part_mix(i + 1, "k", k - 1)
                    low_part_mix(i + 1, "k", K - 1)
                    mix_tokens(i + 1, "r", 0)
                    for k in range(1, K):
                        mix_tokens(i + 1, "r", k)
                        low_part_mix(i + 1, "r", k - 1)
                        combine(i, k - 1)
                    low_part_mix(i + 1, "r", K - 1)
                    combine(i, K - 1)
                else:
                    for m in range(T):
                        combine(i, m)

            nc.vector.memset(xT[:, :, 0:1], 0.0).then_inc(zeroed, 1)
            layernorm_stats(0)
            for n, name in enumerate("krv"):
                dve.wait_ge(w_high, n + 1)
                nc.vector.tensor_tensor(w[name][1][:], w_raw[name][:], w[name][0][:].bitcast(F32),
                                        ALU.subtract).then_inc(w_low, 1)
            dve.wait_ge(small_loaded, 16 * 3)
            dve.wait_ge(zeroed, 1)
            for n in "kr":
                for k in range(K):
                    mix_tokens(0, n, k)
                    low_part_mix(0, n, k)
            dve.wait_ge(gate_ready, 1)
            nc.vector.tensor_scalar(gate[:, 0:1], gate[:, 1:2], 0.5, None, ALU.mult).then_inc(zeroed, 1)
            dve.wait_ge(zeroed, 2)
            iteration(0, True)
            with dve.Fori(1, B - 1) as i:
                iteration(i, True)
            iteration(B - 1, False)

        @block.tensor
        def _(pe):
            def transpose_x(b, m):
                pe.wait_ge(ln_applied, T * b + m + 1)
                wait(pe, xt_copied, T * b + m - 1)
                for k in range(K):
                    last = nc.tensor.transpose(x_ps[m % 2][:, P * k:P * k + P], x_in[:, m, P * k:P * k + P], ident[:])
                last.then_inc(xt_done, 1)

            def project_k(b, g):
                if g == 0:
                    pe.wait_ge(mix_low["k"], K * (b + 1))
                wait(pe, square_done, K * b + g - 1)
                exact_product(nc, k_ps[g % 2][:], lambda k: [part[:, k, P * g:P * g + P] for part in w["k"]],
                              lambda k: [part[:, k, :] for part in mix["k"]], K).then_inc(k_done, 1)

            def project_r(b, m):
                if m == 0:
                    pe.wait_ge(mix_low["r"], K * (b + 1))
                wait(pe, r_ready, T * b + m - 1)
                exact_product(nc, r_ps[m % 2][:], lambda k: [part[:, k, P * m:P * m + P] for part in mix["r"]],
                              lambda k: [part[:, k, :] for part in w["r"]], K).then_inc(r_done, 1)

            def project_v(b, m):
                if m == 0:
                    pe.wait_ge(kact_low, K * (b + 1))
                wait(pe, y_done, T * b + m - 1)
                exact_product(nc, v_ps[m % 2][:], lambda k: [part[:, k, P * m:P * m + P] for part in kact],
                              lambda k: [part[:, k, :] for part in w["v"]], K).then_inc(v_done, 1)

            def iteration(i, has_next):
                for g in range(K):
                    project_k(i, g)
                if has_next:
                    for m in range(T):
                        transpose_x(i + 1, m)
                for m in range(T):
                    project_r(i, m)
                for m in range(T):
                    project_v(i, m)

            pe.wait_ge(pool_const, 2)
            for m in range(T):
                transpose_x(0, m)
            pe.wait_ge(w_low, 3)
            iteration(0, True)
            with pe.Fori(1, B - 1) as i:
                iteration(i, True)
            iteration(B - 1, False)


def build(nc, x, ctxT, mask, g_xattn, g_ffn, wqT, bq, wkT, bk, wvT, bv, woT, bo, w_rT, w_kT, w_vT, mu_r, mu_k, out):
    x1 = nc.dram_tensor("x1", list(x.shape), F32, kind="Internal").ap()
    attention_phase(nc, x, ctxT, mask, g_xattn, wqT, bq, wkT, bk, wvT, bv, woT, bo, x1)
    channel_mix_phase(nc, x1, g_ffn, w_rT, w_kT, w_vT, mu_r, mu_k, out)


def lay_out(inputs):
    a = {n: np.asarray(v) for n, v in inputs.items()}
    D = a["x"].shape[-1]
    K, DH = D // P, D // HEADS

    def tiles(w):
        return np.ascontiguousarray(w.T.reshape(K, P, -1).transpose(1, 0, 2))

    def head_interleaved(v):
        return v.reshape(K, P // DH, DH, -1).swapaxes(1, 2).reshape(D, -1)

    def columns(v):
        return np.ascontiguousarray(v.reshape(K, P).T)

    return {
        "x": np.ascontiguousarray(a["x"]),
        "ctxT": np.ascontiguousarray(a["ctx_1024"].transpose(0, 2, 1)),
        "mask": np.ascontiguousarray(a["mask_BxS2_if1"]),
        "g_xattn": np.ascontiguousarray(a["g_xattn"]),
        "g_ffn": np.ascontiguousarray(a["g_ffn"]),
        "wqT": tiles(head_interleaved(a["L0_xattn_Wq"])),
        "bq": columns(head_interleaved(a["L0_xattn_bq"])),
        "wkT": tiles(head_interleaved(a["L0_xattn_Wk"])),
        "bk": columns(head_interleaved(a["L0_xattn_bk"])),
        "wvT": tiles(a["L0_xattn_Wv"]),
        "bv": columns(a["L0_xattn_bv"]),
        "woT": tiles(a["L0_xattn_Wo"]),
        "bo": np.ascontiguousarray(a["L0_xattn_bo"]),
        "w_rT": tiles(a["L0_ffn_W_r"]),
        "w_kT": tiles(a["L0_ffn_W_k"]),
        "w_vT": tiles(a["L0_ffn_W_v"]),
        "mu_r": columns(a["L0_ffn_mu_r"]),
        "mu_k": columns(a["L0_ffn_mu_k"]),
    }


def kernel(**inputs):
    import concourse.bacc as bacc
    from concourse.bass_utils import run_bass_kernel_spmd

    arrays = lay_out(inputs)
    nc = bacc.Bacc("TRN2", target_bir_lowering=False, num_devices=1)
    args = {n: nc.dram_tensor(f"in_{n}", v.shape, mybir.dt.from_np(v.dtype), kind="ExternalInput").ap()
            for n, v in arrays.items()}
    out = nc.dram_tensor("out_x", arrays["x"].shape, F32, kind="ExternalOutput").ap()
    build(nc, **args, out=out)
    run = run_bass_kernel_spmd(nc, [{f"in_{n}": v for n, v in arrays.items()}], core_ids=[0])
    return run.results[0]["out_x"]
```

```python
from contextlib import ExitStack

import numpy as np

import concourse.bass as bass
from concourse import mybir

ALU = mybir.AluOpType
ACT = mybir.ActivationFunctionType
F32 = mybir.dt.float32
F32R = mybir.dt.float32r
I32 = mybir.dt.int32

P = 128
HEADS = 16
LN_EPS = 1e-5
MASKED = -1e30
RSQRT_SEED = float(0x5F3759DF)


def wait(engine, semaphore, count):
    if not isinstance(count, int) or count > 0:
        engine.wait_ge(semaphore, count)


def stand_alone(engine, semaphore, b):
    if not isinstance(b, int):
        engine.sem_inc(semaphore, 1)


def exact_product(nc, out, stationary, moving, steps, first=True, last=True):
    for n in steps:
        (s_high, s_low), (m_high, m_low) = stationary(n), moving(n)
        nc.tensor.matmul(out, s_high, m_high, start=first and n == steps[0], stop=False)
        nc.tensor.matmul(out, s_high, m_low, start=False, stop=False)
        done = nc.tensor.matmul(out, s_low, m_high, start=False, stop=last and n == steps[-1])
    return done


def attention_phase(nc, x, ctxT, mask, g_xattn, wqT, bq, wkT, bk, wvT, bv, woT, bo, x1):
    B, S, D = x.shape
    H = HEADS
    DH = D // H
    SCALE = float(DH) ** -0.5
    T = S // P
    K = D // P
    HG = P // DH
    PARTS = P // DH
    assert T == 4 and K == 4 and HG == 4 and PARTS == 4

    SEG = [P * t * (t + 1) // 2 for t in range(T + 1)]
    PT_AT = {0: 0, 1: 512, 3: 896, 2: 1024}
    PT_SETS = [[0], [1, 3], [2]]
    PT_COLS = [(0, 512), (512, 1024), (1024, 1280)]

    with ExitStack() as ctx:
        def sb(name, shape, dt=F32):
            return ctx.enter_context(nc.sbuf_tensor(name, shape, dt))

        def psum(name):
            return ctx.enter_context(nc.psum_tensor(name, [P, 512], F32))

        def sem(name):
            return ctx.enter_context(nc.semaphore(name))

        w = {n: [sb(f"w{n}_{part}", [P, K, D], F32R) for part in ("high", "low")] for n in "qkvo"}
        xT = [sb(f"xT_{part}", [P, K, S], F32R) for part in ("high", "low")]
        cT = [sb(f"cT_{part}", [P, K, S], F32R) for part in ("high", "low")]
        x_io = [sb(f"x_io{n}", [P, D]) for n in range(2)]
        tile_in = [sb(f"tile_in{n}", [P, S]) for n in range(2)]
        staged = [sb(f"staged_{part}", [P, S], F32R) for part in ("high", "low")]
        q_stack = [sb(f"q_stack{n}", [P, HG, S], F32R) for n in range(2)]
        k_stack = [sb(f"k_stack{n}", [P, HG, S], F32R) for n in range(2)]
        v = sb("v", [P, T, D])
        probs = sb("probs", [P, 2, SEG[T]])
        probsT = sb("probsT", [P, HG, SEG[T]])
        bias = sb("bias", [P, SEG[T]])
        mask_row = sb("mask_row", [P, S])
        attn = [sb(f"attn_{part}", [P, K, S], F32R) for part in ("high", "low")]
        norm = sb("norm", [P, S])
        bo_gated = sb("bo_gated", [P, D])
        ident = sb("ident", [P, P])
        causal = sb("causal", [P, P])
        columns = sb("columns", [P, 3, K])
        gate = sb("gate", [P, 1])
        least = sb("least", [P, K, T, HG])
        sums = sb("sums", [P, K, T, HG])
        live = sb("live", [P, T, HG])
        inverse = sb("inverse", [P, T, HG])
        stats = sb("stats", [P, T, 6])
        moments = sb("moments", [P, T, 2])
        newton = sb("newton", [P, 3, T])

        score_ps = [psum(f"score_ps{n}") for n in range(2)]
        pt_ps = [psum(f"pt_ps{n}") for n in range(2)]
        proj_ps = [psum(f"proj_ps{n}") for n in range(2)]
        value_ps = psum("value_ps")
        norm_ps = psum("norm_ps")

        w_loaded = {n: sem(f"w{n}_loaded") for n in "qkvo"}
        sp_turns, pool_turns, dve_turns = sem("sp_turns"), sem("pool_turns"), sem("dve_turns")
        w_high = sem("w_high")
        w_low = sem("w_low")
        small_loaded = sem("small_loaded")
        pool_const = sem("pool_const")
        gate_ready = sem("gate_ready")
        x_peeked = [sem(f"x_peeked{n}") for n in range(2)]
        x_loaded = [sem(f"x_loaded{m}") for m in range(T)]
        bn_done = sem("bn_done")
        ln_step = sem("ln_step")
        ln_stats = sem("ln_stats")
        ln_applied = sem("ln_applied")
        xt_done = sem("xt_done")
        xt_high = sem("xt_high")
        xt_low = sem("xt_low")
        c_loaded = [sem(f"c_loaded{n}") for n in range(2)]
        c_high = sem("c_high")
        c_low = sem("c_low")
        q_done, k_done, v_done, o_done = (sem(f"{n}_done") for n in "qkvo")
        q_high, k_high = sem("q_high"), sem("k_high")
        q_low, k_low = sem("q_low"), sem("k_low")
        v_copied = sem("v_copied")
        q_stacked = [sem(f"q_stacked{n}") for n in range(2)]
        k_stacked = [sem(f"k_stacked{n}") for n in range(2)]
        mask_loaded = sem("mask_loaded")
        mask_ready = sem("mask_ready")
        bias_ready = sem("bias_ready")
        scores_done = sem("scores_done")
        scores_read = sem("scores_read")
        exp_done = sem("exp_done")
        pt_done = sem("pt_done")
        pt_act = sem("pt_act")
        pt_dve = sem("pt_dve")
        values_done = sem("values_done")
        inv_step = sem("inv_step")
        norm_spread = sem("norm_spread")
        norm_done = sem("norm_done")
        norm_copied = sem("norm_copied")
        normalised = sem("normalised")
        attn_high = sem("attn_high")
        attn_low = sem("attn_low")
        res_loaded = [sem(f"res_loaded{n}") for n in range(2)]
        res_ready = sem("res_ready")
        o_added = sem("o_added")
        x1_stored = [sem(f"x1_stored{n}") for n in range(2)]

        def room(tensor, n):
            flat = tensor[:].rearrange("p a b -> p (a b)")[:, K * D * n:K * D * (n + 1)]
            return flat.rearrange("p (k n) -> p k n", k=K)

        w_raw = {"q": room(probsT, 0), "k": room(probsT, 1), "v": room(probs, 0), "o": room(probsT, 0)}

        SETS = 3 * H
        TILES = T * H
        LN = 14
        STATS_ORDER = (2, 3, 0, 1)
        BANK = {"v": (0, 1, 0, 1), "q": (0, 0, 0, 0), "o": (1, 1, 0, 1), "k": (1, 1, 0, 0), "x": (1, 1, 0, 1)}

        def proj(kind, n):
            return proj_ps[BANK[kind][n]]

        block = ctx.enter_context(nc.Block())

        def x_tile(m):
            return tile_in[m] if m < 2 else x_io[m - 2]

        def stacked_count(b, g):
            return 64 * (K // 2) * b + 64 * (g // 2 + 1)

        @block.sync
        def _(sp):
            def peek_x(b, n):
                sp.wait_ge(c_low, K * b)
                stand_alone(sp, sp_turns, b)
                sp.dma_start(tile_in[n][:], x[b, P * (n + 2):P * (n + 3)]).then_inc(x_peeked[n], 16)

            def load_x(b, m):
                if m >= 2:
                    wait(sp, x1_stored[m % 2], 32 * (b - 1))
                    wait(sp, xt_done, T * b)
                elif not isinstance(b, int) or b > 0:
                    sp.wait_ge(bn_done, T * b + m + 1)
                stand_alone(sp, sp_turns, b)
                sp.dma_start(x_tile(m)[:], x[b, P * m:P * m + P]).then_inc(x_loaded[m], 16)

            def load_c(b, k):
                if k < 2:
                    sp.wait_ge(xt_done, T * b + k + 1)
                else:
                    sp.wait_ge(c_low, K * b + k - 1)
                stand_alone(sp, sp_turns, b)
                sp.dma_start(tile_in[k % 2][:], ctxT[b, P * k:P * k + P]).then_inc(c_loaded[k % 2], 16)

            def load_mask(b):
                wait(sp, bias_ready, 7 * b)
                stand_alone(sp, sp_turns, b)
                sp.dma_start(mask_row[:].bitcast(I32), mask[b].partition_broadcast(P)).then_inc(mask_loaded, 16)

            def stack(b, g, low_done, stacks, parts, stacked):
                sp.wait_ge(low_done, K * b + g + 1)
                stand_alone(sp, sp_turns, b)
                wait(sp, scores_done, SETS * b + 3 * HG * (g - 1))
                for p in range(PARTS):
                    sp.dma_start(stacks[g % 2][DH * p:DH * p + DH, :, :].bitcast(F32),
                                 staged[parts[p]][:].bitcast(F32)).then_inc(stacked[g % 2], 16)

            def stack_q(b, g):
                stack(b, g, q_low, q_stack, (0, 0, 1, 1), q_stacked)

            def stack_k(b, g):
                stack(b, g, k_low, k_stack, (0, 1, 0, 1), k_stacked)

            def load_residual(b, m, last):
                if m >= 2 or last:
                    sp.wait_ge(x1_stored[m % 2], 32 * b + (16 if m >= 2 else 0))
                else:
                    sp.wait_ge(xt_done, T * (b + 1) + m + 3)
                stand_alone(sp, sp_turns, b)
                sp.dma_start(x_io[m % 2][:], x[b, P * m:P * m + P]).then_inc(res_loaded[m % 2], 16)

            def store_x1(b, m):
                sp.wait_ge(o_added, T * b + m + 1)
                stand_alone(sp, sp_turns, b)
                sp.dma_start(x1[b, P * m:P * m + P], x_io[m % 2][:]).then_inc(x1_stored[m % 2], 16)

            def iteration(i, has_prev, has_next):
                if has_next:
                    peek_x(i + 1, 0)
                    peek_x(i + 1, 1)
                stack_k(i, 1)
                if has_prev:
                    load_residual(i - 1, 0, not has_next)
                    load_residual(i - 1, 1, not has_next)
                if has_next:
                    load_mask(i + 1)
                    load_x(i + 1, 0)
                    load_x(i + 1, 1)
                stack_q(i, 2)
                if has_prev:
                    store_x1(i - 1, 0)
                    load_residual(i - 1, 2, False)
                stack_k(i, 2)
                if has_prev:
                    store_x1(i - 1, 1)
                    load_residual(i - 1, 3, False)
                    store_x1(i - 1, 2)
                if has_next:
                    load_x(i + 1, 2)
                if has_prev:
                    store_x1(i - 1, 3)
                if has_next:
                    load_c(i + 1, 0)
                    load_x(i + 1, 3)
                stack_q(i, 3)
                if has_next:
                    load_c(i + 1, 1)
                stack_k(i, 3)
                if has_next:
                    load_c(i + 1, 2)
                    load_c(i + 1, 3)
                    stack_q(i + 1, 0)
                    stack_k(i + 1, 0)
                    stack_q(i + 1, 1)

            for m in range(T):
                load_x(0, m)
            sp.dma_start(w_raw["q"], wqT).then_inc(w_loaded["q"], 16)
            for k in range(2):
                load_c(0, k)
            sp.dma_start(w_raw["k"], wkT).then_inc(w_loaded["k"], 16)
            for n, col in enumerate((bq, bk, bv)):
                sp.dma_start(columns[:, n, :], col).then_inc(small_loaded, 16)
            sp.dma_start(gate[:], g_xattn.partition_broadcast(P)).then_inc(small_loaded, 16)
            sp.dma_start(bo_gated[:], bo.partition_broadcast(P)).then_inc(small_loaded, 16)
            load_mask(0)
            sp.dma_start(w_raw["v"], wvT).then_inc(w_loaded["v"], 16)
            load_c(0, 2)
            load_c(0, 3)
            sp.wait_ge(w_low, 1)
            sp.dma_start(w_raw["o"], woT).then_inc(w_loaded["o"], 16)
            stack_q(0, 0)
            stack_k(0, 0)
            stack_q(0, 1)
            iteration(0, False, True)
            with sp.Fori(1, B - 1) as i:
                iteration(i, True, True)
            iteration(B - 1, True, False)
            for m in range(2):
                load_residual(B - 1, m, True)
            for m in range(T):
                store_x1(B - 1, m)
                if m < 2:
                    load_residual(B - 1, m + 2, True)
            for n in range(2):
                sp.wait_ge(x1_stored[n], 32 * B)


        @block.gpsimd
        def _(pool):
            def spread_inverse(b, t):
                pool.wait_ge(inv_step, 2 * (K * b + t + 1))
                wait(pool, attn_low, K * b + t)
                stand_alone(pool, pool_turns, b)
                nc.gpsimd.tensor_copy(norm[:].rearrange("p (h d) -> p h d", d=DH),
                                      inverse[:].rearrange("p t h -> p (t h)").unsqueeze(2).broadcast_to([P, T * HG, DH])
                                      ).then_inc(norm_spread, 1)

            def mask_to_bias(b):
                pool.wait_ge(mask_loaded, 16 * (b + 1))
                stand_alone(pool, pool_turns, b)
                nc.gpsimd.tensor_scalar(mask_row[:], mask_row[:].bitcast(I32), 0, MASKED, ALU.is_equal,
                                        ALU.mult).then_inc(mask_ready, 1)

            def add_residual_bias(b, m):
                pool.wait_ge(res_loaded[m % 2], 16 * (T // 2 * b + m // 2 + 1))
                nc.gpsimd.tensor_tensor(x_io[m % 2][:], x_io[m % 2][:], bo_gated[:], ALU.add).then_inc(res_ready, 1)

            def invert_deviation(b):
                at = LN * b
                power, guess, variance = (newton[:, n, :] for n in range(3))
                pool.wait_ge(ln_stats, T * (b + 1))
                wait(pool, ln_applied, T * b)
                stand_alone(pool, pool_turns, b)
                nc.gpsimd.tensor_scalar(variance, moments[:, :, 1], LN_EPS, None, ALU.add).then_inc(ln_step, 1)
                pool.wait_ge(ln_step, at + 1)
                stand_alone(pool, pool_turns, b)
                nc.gpsimd.tensor_scalar(guess.bitcast(I32), variance.bitcast(I32), -0.5, RSQRT_SEED, ALU.mult,
                                        ALU.add).then_inc(ln_step, 1)
                pool.wait_ge(ln_step, at + 2)
                for n in range(3):
                    nc.gpsimd.tensor_tensor(power, guess, guess, ALU.mult).then_inc(ln_step, 1)
                    pool.wait_ge(ln_step, at + 3 + 4 * n)
                    nc.gpsimd.tensor_tensor(power, power, variance, ALU.mult).then_inc(ln_step, 1)
                    pool.wait_ge(ln_step, at + 4 + 4 * n)
                    stand_alone(pool, pool_turns, b)
                    nc.gpsimd.tensor_scalar(power, power, -0.5, 1.5, ALU.mult, ALU.add).then_inc(ln_step, 1)
                    pool.wait_ge(ln_step, at + 5 + 4 * n)
                    nc.gpsimd.tensor_tensor(guess, guess, power, ALU.mult).then_inc(ln_step, 1)
                    pool.wait_ge(ln_step, at + 6 + 4 * n)

            def apply_layernorm(b, m):
                pool.wait_ge(x_loaded[m], 16 * (b + 1))
                stand_alone(pool, pool_turns, b)
                nc.gpsimd.tensor_scalar(x_tile(m)[:], x_tile(m)[:], moments[:, m, 0:1], newton[:, 1, m:m + 1],
                                        ALU.subtract, ALU.mult).then_inc(ln_applied, 1)

            def split_c(b, k):
                pool.wait_ge(c_loaded[k % 2], 16 * (K // 2 * b + k // 2 + 1))
                wait(pool, k_done, K * b)
                stand_alone(pool, pool_turns, b)
                nc.gpsimd.tensor_copy(cT[0][:, k, :], tile_in[k % 2][:]).then_inc(c_high, 1)
                pool.wait_ge(c_high, K * b + k + 1)
                nc.gpsimd.tensor_tensor(cT[1][:, k, :], tile_in[k % 2][:], cT[0][:, k, :].bitcast(F32),
                                        ALU.subtract).then_inc(c_low, 1)

            def iteration(i, has_prev, has_next):
                if has_prev:
                    spread_inverse(i - 1, 3)
                    add_residual_bias(i - 1, 0)
                    add_residual_bias(i - 1, 1)
                if has_next:
                    mask_to_bias(i + 1)
                spread_inverse(i, 0)
                if has_next:
                    invert_deviation(i + 1)
                if has_prev:
                    add_residual_bias(i - 1, 2)
                if has_next:
                    apply_layernorm(i + 1, 0)
                if has_prev:
                    add_residual_bias(i - 1, 3)
                if has_next:
                    apply_layernorm(i + 1, 1)
                spread_inverse(i, 1)
                if has_next:
                    apply_layernorm(i + 1, 2)
                    split_c(i + 1, 0)
                    apply_layernorm(i + 1, 3)
                    for k in range(1, K):
                        split_c(i + 1, k)
                spread_inverse(i, 2)

            nc.gpsimd.memset(ident[:], 0.0).then_inc(pool_const, 1)
            nc.gpsimd.memset(causal[:], 0.0).then_inc(pool_const, 1)
            pool.wait_ge(pool_const, 2)
            nc.gpsimd.affine_select(out=ident[:], in_=ident[:], compare_op=ALU.not_equal, fill=1.0, base=0,
                                    pattern=[[-1, P]], channel_multiplier=1).then_inc(pool_const, 1)
            nc.gpsimd.affine_select(out=causal[:], in_=causal[:], compare_op=ALU.is_ge, fill=MASKED, base=0,
                                    pattern=[[-1, P]], channel_multiplier=1).then_inc(pool_const, 1)
            invert_deviation(0)
            for m in range(T):
                apply_layernorm(0, m)
            for k in range(K):
                split_c(0, k)
            mask_to_bias(0)
            pool.wait_ge(gate_ready, 1)
            nc.gpsimd.tensor_scalar(bo_gated[:], bo_gated[:], gate[:, 0:1], None, ALU.mult).then_inc(pool_const, 1)
            pool.wait_ge(pool_const, 5)
            iteration(0, False, True)
            with pool.Fori(1, B - 1) as i:
                iteration(i, True, True)
            iteration(B - 1, True, False)
            spread_inverse(B - 1, 3)
            for m in range(T):
                add_residual_bias(B - 1, m)

        @block.scalar
        def _(act):
            def high_part_x(b, m):
                act.wait_ge(xt_done, T * b + m + 1)
                wait(act, q_done, K * b)
                nc.scalar.copy(xT[0][:, :, P * m:P * m + P], proj("x", m)[:].rearrange("p (k n) -> p k n", k=K)
                               ).then_inc(xt_high, 1)

            def high_part_q(b, g):
                act.wait_ge(q_done, K * b + g + 1)
                if g > 0:
                    act.wait_ge(k_stacked[(g - 1) % 2], stacked_count(b, g - 1))
                else:
                    wait(act, k_stacked[1], 64 * (K // 2) * b)
                nc.scalar.activation(staged[0][:], proj("q", g)[:], ACT.Identity, bias=columns[:, 0, g:g + 1]
                                     ).then_inc(q_high, 1)

            def high_part_k(b, g):
                act.wait_ge(k_done, K * b + g + 1)
                act.wait_ge(q_stacked[g % 2], stacked_count(b, g))
                nc.scalar.activation(staged[0][:], proj("k", g)[:], ACT.Identity, bias=columns[:, 1, g:g + 1]
                                     ).then_inc(k_high, 1)

            def copy_v(b, m):
                act.wait_ge(v_done, T * b + m + 1)
                wait(act, values_done, K * b)
                nc.scalar.copy(v[:, m, :], proj("v", m)[:]).then_inc(v_copied, 1)

            def copy_norm(b, t):
                act.wait_ge(norm_done, K * b + t + 1)
                nc.scalar.copy(norm[:], norm_ps[:]).then_inc(norm_copied, 1)

            def high_part_attn(b, t):
                act.wait_ge(normalised, K * b + t + 1)
                if t == 0:
                    wait(act, o_done, T * b)
                nc.scalar.activation(attn[0][:, t, :], norm[:], ACT.Identity, bias=columns[:, 2, t:t + 1]
                                     ).then_inc(attn_high, 1)

            def transposed(b, h, n):
                act.wait_ge(pt_done, SETS * b + 3 * h + n + 1)
                wait(act, values_done, K * b + h // HG)
                lo, hi = PT_COLS[n]
                nc.scalar.copy(probsT[:, h % HG, lo:hi], pt_ps[n % 2][:, 0:hi - lo]).then_inc(pt_act, 1)

            def exponent(b, h, t):
                act.wait_ge(scores_read, TILES * b + T * h + t + 1)
                here = probs[:, h % 2, SEG[t]:SEG[t + 1]]
                at = (h // HG, t, h % HG)
                nc.scalar.activation(here, here, ACT.Exp, bias=least[:, at[0], at[1], at[2]:at[2] + 1], scale=-1.0,
                                     accum_out=sums[:, at[0], at[1], at[2]:at[2] + 1]).then_inc(exp_done, 1)

            def after(i, s, has_prev, has_next):
                if s == 0:
                    high_part_k(i, 1)
                    copy_v(i, 0)
                if s == 1:
                    copy_v(i, 1)
                    if has_prev:
                        high_part_attn(i - 1, 3)
                    copy_v(i, 2)
                if s == 2:
                    copy_v(i, 3)
                    high_part_q(i, 2)
                if s == 4:
                    high_part_k(i, 2)
                if s == 7:
                    high_part_attn(i, 0)
                if s == 8:
                    high_part_q(i, 3)
                if s == 9:
                    high_part_k(i, 3)
                if 8 <= s <= 10 and has_next:
                    high_part_x(i + 1, s - 8)
                if s == 10 and has_next:
                    high_part_x(i + 1, 3)
                if s == 10:
                    high_part_attn(i, 1)
                if s == 12 and has_next:
                    high_part_q(i + 1, 0)
                if s == 13 and has_next:
                    high_part_k(i + 1, 0)
                if s == 14:
                    high_part_attn(i, 2)
                    if has_next:
                        high_part_q(i + 1, 1)

            def iteration(i, has_prev, has_next):
                for s in range(H):
                    before = (i, s - 1) if s > 0 else (i - 1, H - 1)
                    exponent(i, s, 0)
                    exponent(i, s, 1)
                    if s > 0 or has_prev:
                        transposed(*before, 0)
                    if s % HG == 1 and (s > 1 or has_prev):
                        copy_norm(*((i, s // HG - 1) if s > 1 else (i - 1, K - 1)))
                    exponent(i, s, 2)
                    exponent(i, s, 3)
                    if s > 0 or has_prev:
                        transposed(*before, 2)
                    after(i, s, has_prev, has_next)

            def split_weights(n, name):
                act.wait_ge(w_loaded[name], 16)
                nc.scalar.copy(w[name][0][:], w_raw[name]).then_inc(w_high, 1)

            for m in range(T):
                high_part_x(0, m)
            split_weights(0, "q")
            split_weights(1, "k")
            act.wait_ge(small_loaded, 16 * 5)
            high_part_q(0, 0)
            high_part_k(0, 0)
            split_weights(2, "v")
            high_part_q(0, 1)
            nc.scalar.activation(gate[:], gate[:], ACT.Tanh).then_inc(gate_ready, 1)
            split_weights(3, "o")
            iteration(0, False, True)
            with act.Fori(1, B - 1) as i:
                iteration(i, True, True)
            iteration(B - 1, True, False)
            for n in (0, 2):
                transposed(B - 1, H - 1, n)
            copy_norm(B - 1, 3)
            high_part_attn(B - 1, 3)

        @block.vector
        def _(dve):
            def layernorm_stats(b, n):
                m = STATS_ORDER[n]
                if m < 2 or isinstance(b, int) and b == 0:
                    dve.wait_ge(x_loaded[m], 16 * (b + 1))
                    tile = x_tile(m)
                else:
                    dve.wait_ge(x_peeked[m - 2], 16 * b)
                    tile = tile_in[m - 2]
                wait(dve, ln_stats, T * b)
                nc.vector.bn_stats(stats[:, m, :], tile[:]).then_inc(bn_done, 1)

            def aggregate_stats(b):
                dve.wait_ge(bn_done, T * (b + 1))
                wait(dve, ln_applied, T * b)
                stand_alone(dve, dve_turns, b)
                for m in range(T):
                    nc.vector.bn_aggr(moments[:, m, :], stats[:, m, :]).then_inc(ln_stats, 1)

            def low_part_x(b, m):
                dve.wait_ge(xt_high, T * b + m + 1)
                nc.vector.tensor_tensor(xT[1][:, :, P * m:P * m + P], proj("x", m)[:].rearrange("p (k n) -> p k n", k=K),
                                        xT[0][:, :, P * m:P * m + P].bitcast(F32), ALU.subtract).then_inc(xt_low, 1)

            def low_part_q(b, g):
                dve.wait_ge(q_high, K * b + g + 1)
                nc.vector.scalar_tensor_tensor(out=staged[1][:], in0=proj("q", g)[:], scalar=columns[:, 0, g:g + 1],
                                               in1=staged[0][:].bitcast(F32), op0=ALU.add, op1=ALU.subtract
                                               ).then_inc(q_low, 1)

            def low_part_k(b, g):
                dve.wait_ge(k_high, K * b + g + 1)
                nc.vector.scalar_tensor_tensor(out=staged[1][:], in0=proj("k", g)[:], scalar=columns[:, 1, g:g + 1],
                                               in1=staged[0][:].bitcast(F32), op0=ALU.add, op1=ALU.subtract
                                               ).then_inc(k_low, 1)

            def build_bias(b, t):
                dve.wait_ge(mask_ready, b + 1)
                wait(dve, scores_read, TILES * b - (T - 1 - t))
                nc.vector.tensor_tensor(bias[:, SEG[t + 1] - P:SEG[t + 1]], mask_row[:, P * t:P * t + P], causal[:],
                                        ALU.add).then_inc(bias_ready, 1)
                if t > 0:
                    nc.vector.tensor_copy(bias[:, SEG[t]:SEG[t + 1] - P], mask_row[:, 0:P * t]).then_inc(bias_ready, 1)

            def bias_scores(b, h, t):
                c = max(t - 1, 0)
                if h == 0:
                    dve.wait_ge(bias_ready, 7 * b + 2 * t + 1)
                if t != 1:
                    dve.wait_ge(scores_done, SETS * b + 3 * h + c + 1)
                    if t == 0:
                        wait(dve, pt_done, SETS * b + 3 * (h - 1))
                if t != 1 or h == 0:
                    stand_alone(dve, dve_turns, b)
                at = P if t == 1 else 0
                width = P * (t + 1)
                nc.vector.tensor_tensor_reduce(
                    out=probs[:, h % 2, SEG[t]:SEG[t + 1]], in0=score_ps[(h + c) % 2][:, at:at + width],
                    in1=bias[:, SEG[t]:SEG[t + 1]], scale=-SCALE, scalar=3e38, op0=ALU.add, op1=ALU.min,
                    accum_out=least[:, h // HG, t, h % HG:h % HG + 1]).then_inc(scores_read, 1)

            def transposed(b, h):
                dve.wait_ge(pt_done, SETS * b + 3 * h + 2)
                wait(dve, values_done, K * b + h // HG)
                lo, hi = PT_COLS[1]
                nc.vector.tensor_copy(probsT[:, h % HG, lo:hi], pt_ps[1][:, 0:hi - lo]).then_inc(pt_dve, 1)

            def invert_sums(b, t):
                dve.wait_ge(exp_done, TILES * b + T * HG * (t + 1))
                nc.vector.scalar_tensor_tensor(out=live[:], in0=least[:, t], scalar=-MASKED / 100, in1=sums[:, t],
                                               op0=ALU.is_lt, op1=ALU.mult).then_inc(inv_step, 1)
                dve.wait_ge(inv_step, 2 * (K * b + t) + 1)
                wait(dve, norm_spread, K * b + t)
                nc.vector.reciprocal(inverse[:], live[:]).then_inc(inv_step, 1)

            def normalise(b, t):
                dve.wait_ge(norm_copied, K * b + t + 1)
                dve.wait_ge(values_done, K * b + t + 1)
                nc.vector.tensor_tensor(norm[:], value_ps[:], norm[:], ALU.mult).then_inc(normalised, 1)

            def low_part_attn(b, t):
                dve.wait_ge(attn_high, K * b + t + 1)
                nc.vector.scalar_tensor_tensor(out=attn[1][:, t, :], in0=norm[:], scalar=columns[:, 2, t:t + 1],
                                               in1=attn[0][:, t, :].bitcast(F32), op0=ALU.add, op1=ALU.subtract
                                               ).then_inc(attn_low, 1)

            def add_output(b, m):
                dve.wait_ge(o_done, T * b + m + 1)
                dve.wait_ge(res_ready, T * b + m + 1)
                nc.vector.scalar_tensor_tensor(out=x_io[m % 2][:], in0=proj("o", m)[:], scalar=gate[:, 0:1],
                                               in1=x_io[m % 2][:], op0=ALU.mult, op1=ALU.add).then_inc(o_added, 1)

            def between(i, s, has_prev, has_next):
                if s == 0 and has_prev:
                    invert_sums(i - 1, 3)
                if s == 1:
                    low_part_k(i, 1)
                    if has_prev:
                        normalise(i - 1, 3)
                if s == 2 and has_prev:
                    low_part_attn(i - 1, 3)
                if s == 3:
                    low_part_q(i, 2)
                if s == 4:
                    if has_prev:
                        add_output(i - 1, 0)
                    invert_sums(i, 0)
                if s == 5:
                    low_part_k(i, 2)
                if s == 6:
                    normalise(i, 0)
                    if has_prev:
                        add_output(i - 1, 1)
                if s == 7 and has_prev:
                    add_output(i - 1, 2)
                if s == 8:
                    if has_prev:
                        add_output(i - 1, 3)
                    low_part_attn(i, 0)
                    invert_sums(i, 1)
                if s == 9:
                    low_part_q(i, 3)
                if s == 10:
                    low_part_k(i, 3)
                if 9 <= s <= 11 and has_next:
                    low_part_x(i + 1, s - 9)
                if s == 11 and has_next:
                    low_part_x(i + 1, 3)
                if s == 10:
                    normalise(i, 1)
                if s == 11:
                    low_part_attn(i, 1)
                if s == 12:
                    invert_sums(i, 2)
                if s == 13 and has_next:
                    low_part_q(i + 1, 0)
                if s == 14:
                    normalise(i, 2)
                    if has_next:
                        low_part_k(i + 1, 0)
                if s == 15:
                    low_part_attn(i, 2)
                    if has_next:
                        low_part_q(i + 1, 1)

            def iteration(i, has_prev, has_next):
                for s in range(H):
                    rebuild = has_next and s == H - 1
                    for t in range(3):
                        bias_scores(i, s, t)
                        if rebuild and t > 0:
                            build_bias(i + 1, t - 1)
                    between(i, s, has_prev, has_next)
                    bias_scores(i, s, 3)
                    if rebuild:
                        build_bias(i + 1, 2)
                        build_bias(i + 1, 3)
                    if s > 0:
                        transposed(i, s - 1)
                    elif has_prev:
                        transposed(i - 1, H - 1)
                    if s < 4 and has_next:
                        layernorm_stats(i + 1, s)
                        if s == 3:
                            aggregate_stats(i + 1)

            def split_weights(n, name):
                dve.wait_ge(w_high, n + 1)
                nc.vector.tensor_tensor(w[name][1][:], w_raw[name], w[name][0][:].bitcast(F32),
                                        ALU.subtract).then_inc(w_low, 1)

            for n in range(T):
                layernorm_stats(0, n)
            aggregate_stats(0)
            for m in range(T):
                low_part_x(0, m)
            split_weights(0, "q")
            split_weights(1, "k")
            low_part_q(0, 0)
            low_part_k(0, 0)
            split_weights(2, "v")
            low_part_q(0, 1)
            split_weights(3, "o")
            dve.wait_ge(w_low, 4)
            dve.wait_ge(pool_const, 5)
            for t in range(T):
                build_bias(0, t)
            iteration(0, False, True)
            with dve.Fori(1, B - 1) as i:
                iteration(i, True, True)
            iteration(B - 1, True, False)
            transposed(B - 1, H - 1)
            invert_sums(B - 1, 3)
            normalise(B - 1, 3)
            low_part_attn(B - 1, 3)
            for m in range(T):
                add_output(B - 1, m)

        @block.tensor
        def _(pe):
            def scores(b, h, c):
                g, j = h // HG, h % HG
                if j == 0 and c == 0:
                    pe.wait_ge(q_stacked[g % 2], stacked_count(b, g))
                    pe.wait_ge(k_stacked[g % 2], stacked_count(b, g))
                wait(pe, scores_read, TILES * b + T * h + (-1, 0, 2)[c])
                bank = score_ps[(h + c) % 2]
                for t in ((0, 1), (2,), (3,))[c]:
                    at = P if t == 1 else 0
                    last = nc.tensor.matmul(bank[:, at:at + P * (t + 1)], q_stack[g % 2][:, j, P * t:P * t + P],
                                            k_stack[g % 2][:, j, 0:P * (t + 1)], start=True, stop=True)
                last.then_inc(scores_done, 1)

            def transpose_probs(b, h, n):
                if n == 0:
                    pe.wait_ge(exp_done, TILES * b + T * (h + 1))
                if n == 1:
                    wait(pe, pt_dve, H * b + h)
                else:
                    wait(pe, pt_act, 2 * (H * b + h) + n // 2)
                for k in PT_SETS[n]:
                    for t in range(k, T):
                        at = PT_AT[k] - PT_COLS[n][0] + P * (t - k)
                        last = nc.tensor.transpose(pt_ps[n % 2][:, at:at + P],
                                                   probs[:, h % 2, SEG[t] + P * k:SEG[t] + P * k + P], ident[:])
                last.then_inc(pt_done, 1)

            def transpose_inverse(b, t):
                pe.wait_ge(norm_spread, K * b + t + 1)
                wait(pe, norm_copied, K * b + t)
                for n in range(T):
                    last = nc.tensor.transpose(norm_ps[:, P * n:P * n + P], norm[:, P * n:P * n + P], ident[:])
                last.then_inc(norm_done, 1)

            def values(b, t):
                pe.wait_ge(pt_act, 2 * H * b + 2 * HG * (t + 1))
                pe.wait_ge(pt_dve, H * b + HG * (t + 1))
                if t == 0:
                    pe.wait_ge(v_copied, T * (b + 1))
                wait(pe, normalised, K * b + t)
                for k in range(T):
                    for j in range(HG):
                        last = nc.tensor.matmul(value_ps[DH * j:DH * j + DH, P * k:S],
                                                v[:, k, P * t + DH * j:P * t + DH * j + DH],
                                                probsT[:, j, PT_AT[k]:PT_AT[k] + S - P * k],
                                                start=(k == 0), stop=(k == T - 1), skip_group_check=True)
                last.then_inc(values_done, 1)

            def product(kind, n, k, stationary, moving, done):
                last = exact_product(nc, proj(kind, n)[:], stationary, moving, [k], k == 0, k == K - 1)
                if k == K - 1:
                    last.then_inc(done, 1)

            def project_q(b, g, k, has_prev=True):
                if k == 0 and g == 0:
                    pe.wait_ge(xt_low, T * (b + 1))
                elif k == 0 and g == 1:
                    pe.wait_ge(q_low, K * b + 1)
                elif k == 0 and g == 2:
                    pe.wait_ge(v_copied, T * b + 3)
                elif k == 0 and has_prev:
                    pe.wait_ge(o_added, T * b - 1)
                elif k == 0:
                    pe.wait_ge(k_low, K * b + 3)
                product("q", g, k, lambda k: [part[:, k, P * g:P * g + P] for part in w["q"]],
                        lambda k: [part[:, k, :] for part in xT], q_done)

            def project_k(b, g, k):
                if k == 0 and g == 0:
                    pe.wait_ge(c_low, K * (b + 1))
                    pe.wait_ge(xt_low, T * (b + 1))
                elif k == 0 and g == 1:
                    pe.wait_ge(k_low, K * b + 1)
                elif k == 0:
                    pe.wait_ge(q_low, K * b + g + 1)
                product("k", g, k, lambda k: [part[:, k, P * g:P * g + P] for part in w["k"]],
                        lambda k: [part[:, k, :] for part in cT], k_done)

            def project_v(b, m, k):
                if k == 0 and m == 0:
                    pe.wait_ge(q_low, K * b + 2)
                elif k == 0 and m == 1:
                    pe.wait_ge(k_low, K * b + 2)
                elif k == 0:
                    pe.wait_ge(v_copied, T * b + m - 1)
                product("v", m, k, lambda k: [part[:, k, P * m:P * m + P] for part in cT],
                        lambda k: [part[:, k, :] for part in w["v"]], v_done)

            def project_o(b, m, k, has_next=True):
                if k == 0 and m == 0:
                    pe.wait_ge(attn_low, K * (b + 1))
                    if has_next:
                        pe.wait_ge(v_copied, T * (b + 2))
                elif k == 0 and m == 2 and has_next:
                    pe.wait_ge(k_low, K * (b + 1) + 3)
                elif k == 0 and m == 2:
                    pe.wait_ge(k_low, K * (b + 1))
                elif k == 0:
                    pe.wait_ge(o_added, T * b + (1 if m == 1 else 2))
                product("o", m, k, lambda k: [part[:, k, P * m:P * m + P] for part in attn],
                        lambda k: [part[:, k, :] for part in w["o"]], o_done)

            def transpose_x(b, m):
                pe.wait_ge(ln_applied, T * b + m + 1)
                if m == 0:
                    wait(pe, v_copied, T * b)
                    wait(pe, o_added, T * (b - 1))
                elif m == 2:
                    wait(pe, k_low, K * b)
                else:
                    pe.wait_ge(xt_low, T * b + (1 if m == 1 else 2))
                for k in range(K):
                    last = nc.tensor.transpose(proj("x", m)[:, P * k:P * k + P], x_tile(m)[:, P * k:P * k + P], ident[:])
                last.then_inc(xt_done, 1)

            NOW = {0: "v0", 1: "v1 v2", 2: "v3 q2", 4: "k2", 8: "q3", 9: "k3"}
            PREV = {3: "o0", 5: "o1", 6: "o2", 7: "o3"}
            NEXT = {12: "q0", 13: "k0", 14: "q1", 15: "k1"}
            LATE = (1, 9)

            def project(i, s, has_prev, has_next, third):
                pieces = [(i - 1, x) for x in PREV.get(s, "").split()] if has_prev else []
                pieces += [(i, x) for x in NOW.get(s, "").split()]
                if has_next:
                    pieces += [(i + 1, x) for x in NEXT.get(s, "").split()]
                steps = [(b, x, k) for b, x in pieces for k in range(K)]
                shares = (0, 0, 2, 4) if s in LATE else (0, 1, 2, 4)
                a, z = (len(steps) * share // 4 for share in shares[third:third + 2])
                for b, x, k in steps[a:z]:
                    n = int(x[1])
                    if x[0] == "q":
                        project_q(b, n, k, has_prev)
                    elif x[0] == "k":
                        project_k(b, n, k)
                    elif x[0] == "v":
                        project_v(b, n, k)
                    else:
                        project_o(b, n, k)

            def iteration(i, has_prev, has_next):
                for s in range(H):
                    before = (i, s - 1) if s > 0 else (i - 1, H - 1)
                    scores(i, s, 0)
                    scores(i, s, 1)
                    project(i, s, has_prev, has_next, 0)
                    if s > 0 or has_prev:
                        transpose_probs(*before, 0)
                    scores(i, s, 2)
                    project(i, s, has_prev, has_next, 1)
                    if s > 0 or has_prev:
                        transpose_probs(*before, 1)
                    if s % HG == 0 and (s > 0 or has_prev):
                        transpose_probs(*before, 2)
                        project(i, s, has_prev, has_next, 2)
                    else:
                        project(i, s, has_prev, has_next, 2)
                        if s > 0 or has_prev:
                            transpose_probs(*before, 2)
                    if 8 <= s <= 10 and has_next:
                        transpose_x(i + 1, s - 8)
                    if s == 10 and has_next:
                        transpose_x(i + 1, 3)
                    if s % HG == 0 and (s > 0 or has_prev):
                        group = (i, s // HG - 1) if s > 0 else (i - 1, K - 1)
                        values(*group)
                        transpose_inverse(*group)

            pe.wait_ge(pool_const, 4)
            for m in range(T):
                transpose_x(0, m)
            pe.wait_ge(w_low, 1)
            for k in range(K):
                project_q(0, 0, k)
            pe.wait_ge(w_low, 2)
            for k in range(K):
                project_k(0, 0, k)
            for k in range(K):
                project_q(0, 1, k)
            for k in range(K):
                project_k(0, 1, k)
            pe.wait_ge(w_low, 3)
            iteration(0, False, True)
            with pe.Fori(1, B - 1) as i:
                iteration(i, True, True)
            iteration(B - 1, True, False)
            for n in range(3):
                transpose_probs(B - 1, H - 1, n)
            values(B - 1, K - 1)
            transpose_inverse(B - 1, K - 1)
            for m in range(T):
                for k in range(K):
                    project_o(B - 1, m, k, False)


def channel_mix_phase(nc, x1, g_ffn, wrT, wkT, wvT, mu_r, mu_k, out):
    B, S, D = x1.shape
    T = S // P
    K = D // P

    with ExitStack() as ctx:
        def sb(name, shape, dt=F32):
            return ctx.enter_context(nc.sbuf_tensor(name, shape, dt))

        def psums(name, n):
            return [ctx.enter_context(nc.psum_tensor(f"{name}{i}", [P, 512], F32)) for i in range(n)]

        def sem(name):
            return ctx.enter_context(nc.semaphore(name))

        def pair(name):
            return [sb(f"{name}_{part}", [P, K, S], F32R) for part in ("high", "low")]

        w = {n: pair(f"ffn_w{n}") for n in "krv"}
        w_raw = {"k": sb("ffn_raw_k", [P, K, D]), "r": sb("ffn_raw_r", [P, K, D])}
        w_raw["v"] = w_raw["k"]
        x_in = sb("ffn_x_in", [P, T, D])
        xT = sb("ffn_xT", [P, K, S + 1])
        delta = sb("delta", [P, K, S])
        mixed = {n: sb(f"mixed_{n}", [P, 2, S]) for n in "kr"}
        mix = {n: pair(f"mix_{n}") for n in "kr"}
        relu = sb("relu", [P, 2, S])
        square = sb("square", [P, 2, S])
        kact = pair("kact")
        r_tanh = sb("r_tanh", [P, T, D])
        y = sb("y", [P, 2, D])
        res = sb("res", [P, T, D])
        ident = sb("ffn_ident", [P, P])
        mu = sb("mu", [P, 2, K])
        gate = sb("ffn_gate", [P, 2])
        stats = sb("ffn_stats", [P, T, 6])
        moments = sb("ffn_moments", [P, T, 2])
        rstd = sb("ffn_rstd", [P, T])
        newton = sb("ffn_newton", [P, 3, T])

        x_ps, k_ps, r_ps, v_ps = psums("ffn_x_ps", 2), psums("ffn_k_ps", 2), psums("ffn_r_ps", 2), psums("ffn_v_ps", 2)

        w_loaded = {n: sem(f"ffn_w{n}_loaded") for n in "krv"}
        sp_turns, pool_turns, dve_turns = sem("ffn_sp_turns"), sem("ffn_pool_turns"), sem("ffn_dve_turns")
        w_high, w_low = sem("ffn_w_high"), sem("ffn_w_low")
        small_loaded, gate_ready, pool_const = sem("ffn_small"), sem("ffn_gate_ready"), sem("ffn_pool_const")
        zeroed = sem("zeroed")
        x_loaded = sem("ffn_x_loaded")
        ln_step = sem("ffn_ln_step")
        ln_stats = sem("ffn_ln_stats")
        ln_applied = sem("ffn_ln_applied")
        xt_done = sem("ffn_xt_done")
        xt_copied = sem("ffn_xt_copied")
        delta_done = sem("delta_done")
        mixed_done = {n: sem(f"mixed_{n}_done") for n in "kr"}
        mix_high = {n: sem(f"mix_{n}_high") for n in "kr"}
        mix_low = {n: sem(f"mix_{n}_low") for n in "kr"}
        k_done, r_done, v_done = sem("ffn_k_done"), sem("ffn_r_done"), sem("ffn_v_done")
        relu_done, square_done = sem("relu_done"), sem("square_done")
        kact_high, kact_low = sem("kact_high"), sem("kact_low")
        r_ready = sem("r_ready")
        y_done, added = sem("y_done"), sem("added")
        res_loaded = [sem(f"ffn_res_loaded{m}") for m in range(T)]
        stored = [sem(f"ffn_stored{m}") for m in range(T)]

        LN = T + T + 10
        block = ctx.enter_context(nc.Block())

        @block.sync
        def _(sp):
            def load_x(b):
                wait(sp, xt_done, T * b)
                stand_alone(sp, sp_turns, b)
                sp.dma_start(x_in[:], x1[b].rearrange("(t p) d -> p t d", p=P)).then_inc(x_loaded, 16)

            def load_res(b, m):
                wait(sp, stored[m], 16 * b)
                stand_alone(sp, sp_turns, b)
                sp.dma_start(res[:, m, :], x1[b, P * m:P * m + P]).then_inc(res_loaded[m], 16)

            def store(b, m):
                sp.wait_ge(added, T * b + m + 1)
                stand_alone(sp, sp_turns, b)
                sp.dma_start(out[b, P * m:P * m + P], res[:, m, :]).then_inc(stored[m], 16)

            def iteration(i, has_next):
                for m in range(T):
                    load_res(i, m)
                if has_next:
                    load_x(i + 1)
                for m in range(T):
                    store(i, m)

            load_x(0)
            sp.dma_start(w_raw["k"][:], wkT).then_inc(w_loaded["k"], 16)
            sp.dma_start(w_raw["r"][:], wrT).then_inc(w_loaded["r"], 16)
            sp.dma_start(mu[:, 0, :], mu_k).then_inc(small_loaded, 16)
            sp.dma_start(mu[:, 1, :], mu_r).then_inc(small_loaded, 16)
            sp.dma_start(gate[:, 0:1], g_ffn.partition_broadcast(P)).then_inc(small_loaded, 16)
            sp.wait_ge(w_low, 1)
            sp.dma_start(w_raw["v"][:], wvT).then_inc(w_loaded["v"], 16)
            iteration(0, True)
            with sp.Fori(1, B - 1) as i:
                iteration(i, True)
            iteration(B - 1, False)
            for m in range(T):
                sp.wait_ge(stored[m], 16 * B)

        @block.gpsimd
        def _(pool):
            def apply_layernorm(b, m):
                pool.wait_ge(ln_stats, b + 1)
                stand_alone(pool, pool_turns, b)
                nc.gpsimd.tensor_scalar(x_in[:, m, :], x_in[:, m, :], moments[:, m, 0:1], rstd[:, m:m + 1],
                                        ALU.subtract, ALU.mult).then_inc(ln_applied, 1)

            def take_delta(b, k):
                pool.wait_ge(xt_copied, T * (b + 1))
                nc.gpsimd.tensor_tensor(delta[:, k, :], xT[:, k, 1:S + 1], xT[:, k, 0:S], ALU.subtract).then_inc(delta_done, 1)

            def low_part_act(b, k):
                pool.wait_ge(kact_high, K * b + k + 1)
                nc.gpsimd.tensor_tensor(kact[1][:, k, :], square[:, k % 2, :], kact[0][:, k, :].bitcast(F32),
                                        ALU.subtract).then_inc(kact_low, 1)

            def iteration(i, has_next):
                if has_next:
                    apply_layernorm(i + 1, 0)
                low_part_act(i, 0)
                if has_next:
                    apply_layernorm(i + 1, 1)
                low_part_act(i, 1)
                if has_next:
                    apply_layernorm(i + 1, 2)
                low_part_act(i, 2)
                if has_next:
                    apply_layernorm(i + 1, 3)
                low_part_act(i, 3)
                if has_next:
                    for k in range(K):
                        take_delta(i + 1, k)

            nc.gpsimd.memset(ident[:], 0.0).then_inc(pool_const, 1)
            pool.wait_ge(pool_const, 1)
            nc.gpsimd.affine_select(out=ident[:], in_=ident[:], compare_op=ALU.not_equal, fill=1.0, base=0,
                                    pattern=[[-1, P]], channel_multiplier=1).then_inc(pool_const, 1)
            for m in range(T):
                apply_layernorm(0, m)
            pool.wait_ge(zeroed, 1)
            for k in range(K):
                take_delta(0, k)
            iteration(0, True)
            with pool.Fori(1, B - 1) as i:
                iteration(i, True)
            iteration(B - 1, False)

        @block.scalar
        def _(act):
            def copy_x(b, m):
                act.wait_ge(xt_done, T * b + m + 1)
                wait(act, mixed_done["r"], K * b)
                nc.scalar.copy(xT[:, :, 1 + P * m:1 + P * m + P], x_ps[m % 2][:].rearrange("p (k n) -> p k n", k=K)
                               ).then_inc(xt_copied, 1)

            def high_part_mix(b, n, k, done):
                act.wait_ge(mixed_done[n], K * b + k + 1)
                wait(act, done, K * b)
                nc.scalar.copy(mix[n][0][:, k, :], mixed[n][:, k % 2, :]).then_inc(mix_high[n], 1)

            def relu_k(b, k):
                act.wait_ge(k_done, K * b + k + 1)
                wait(act, square_done, K * b + k - 1)
                nc.scalar.activation(relu[:, k % 2, :], k_ps[k % 2][:], ACT.Relu).then_inc(relu_done, 1)

            def high_part_act(b, k):
                act.wait_ge(square_done, K * b + k + 1)
                wait(act, v_done, T * b)
                nc.scalar.copy(kact[0][:, k, :], square[:, k % 2, :]).then_inc(kact_high, 1)

            def gate_r(b, m):
                act.wait_ge(r_done, T * b + m + 1)
                wait(act, y_done, T * (b - 1) + m + 1)
                nc.scalar.activation(r_tanh[:, m, :], r_ps[m % 2][:], ACT.Tanh, scale=0.5).then_inc(r_ready, 1)

            def iteration(i, has_next):
                relu_k(i, 0)
                for k in range(1, K):
                    relu_k(i, k)
                    high_part_act(i, k - 1)
                high_part_act(i, K - 1)
                for m in range(T):
                    if has_next:
                        copy_x(i + 1, m)
                for m in range(T):
                    gate_r(i, m)
                    if has_next:
                        high_part_mix(i + 1, "k", m, k_done)
                if has_next:
                    for k in range(K):
                        high_part_mix(i + 1, "r", k, r_done)

            for m in range(T):
                copy_x(0, m)
            for n, name in enumerate("krv"):
                act.wait_ge(w_loaded[name], 16)
                nc.scalar.copy(w[name][0][:], w_raw[name][:]).then_inc(w_high, 1)
            for n, done in (("k", k_done), ("r", r_done)):
                for k in range(K):
                    high_part_mix(0, n, k, done)
            act.wait_ge(small_loaded, 16 * 3)
            nc.scalar.activation(gate[:, 1:2], gate[:, 0:1], ACT.Tanh).then_inc(gate_ready, 1)
            iteration(0, True)
            with act.Fori(1, B - 1) as i:
                iteration(i, True)
            iteration(B - 1, False)

        @block.vector
        def _(dve):
            def layernorm_stats(b):
                at = LN * b
                dve.wait_ge(x_loaded, 16 * (b + 1))
                wait(dve, ln_applied, T * b)
                wait(dve, ln_stats, b)
                for m in range(T):
                    nc.vector.bn_stats(stats[:, m, :], x_in[:, m, :]).then_inc(ln_step, 1)
                dve.wait_ge(ln_step, at + T)
                stand_alone(dve, dve_turns, b)
                for m in range(T):
                    nc.vector.bn_aggr(moments[:, m, :], stats[:, m, :]).then_inc(ln_step, 1)
                dve.wait_ge(ln_step, at + 2 * T)
                variance, guess, power = newton[:, 0, :], newton[:, 1, :], newton[:, 2, :]
                at += 2 * T
                nc.vector.tensor_scalar(variance, moments[:, :, 1], LN_EPS, None, ALU.add).then_inc(ln_step, 1)
                dve.wait_ge(ln_step, at + 1)
                nc.vector.tensor_scalar(guess.bitcast(I32), variance.bitcast(I32), -0.5, RSQRT_SEED, ALU.mult,
                                        ALU.add).then_inc(ln_step, 1)
                dve.wait_ge(ln_step, at + 2)
                for n in range(3):
                    nc.vector.tensor_tensor(power, guess, guess, ALU.mult).then_inc(ln_step, 1)
                    dve.wait_ge(ln_step, at + 3 + 3 * n)
                    nc.vector.scalar_tensor_tensor(out=power, in0=power, scalar=-0.5, in1=variance, op0=ALU.mult,
                                                   op1=ALU.mult).then_inc(ln_step, 1)
                    dve.wait_ge(ln_step, at + 4 + 3 * n)
                    step = nc.vector.scalar_tensor_tensor(out=rstd[:] if n == 2 else guess, in0=power, scalar=1.5,
                                                          in1=guess, op0=ALU.add, op1=ALU.mult)
                    if n < 2:
                        step.then_inc(ln_step, 1)
                        dve.wait_ge(ln_step, at + 5 + 3 * n)
                    else:
                        step.then_inc(ln_stats, 1)

            def mix_tokens(b, n, k):
                dve.wait_ge(delta_done, K * b + k + 1)
                wait(dve, mix_low[n], K * b + k - 1)
                col = "kr".index(n)
                nc.vector.scalar_tensor_tensor(out=mixed[n][:, k % 2, :], in0=delta[:, k, :], scalar=mu[:, col, k:k + 1],
                                               in1=xT[:, k, 0:S], op0=ALU.mult, op1=ALU.add).then_inc(mixed_done[n], 1)

            def low_part_mix(b, n, k):
                dve.wait_ge(mix_high[n], K * b + k + 1)
                nc.vector.tensor_tensor(mix[n][1][:, k, :], mixed[n][:, k % 2, :], mix[n][0][:, k, :].bitcast(F32),
                                        ALU.subtract).then_inc(mix_low[n], 1)

            def square_k(b, k):
                dve.wait_ge(relu_done, K * b + k + 1)
                wait(dve, kact_low, K * b + k - 1)
                nc.vector.scalar_tensor_tensor(out=square[:, k % 2, :], in0=k_ps[k % 2][:], scalar=0.0,
                                               in1=relu[:, k % 2, :], op0=ALU.max, op1=ALU.mult).then_inc(square_done, 1)

            def combine(b, m):
                dve.wait_ge(v_done, T * b + m + 1)
                dve.wait_ge(r_ready, T * b + m + 1)
                wait(dve, added, T * b + m - 1)
                nc.vector.scalar_tensor_tensor(out=y[:, m % 2, :], in0=r_tanh[:, m, :], scalar=1.0, in1=v_ps[m % 2][:],
                                               op0=ALU.add, op1=ALU.mult).then_inc(y_done, 1)
                dve.wait_ge(y_done, T * b + m + 1)
                dve.wait_ge(res_loaded[m], 16 * (b + 1))
                nc.vector.scalar_tensor_tensor(out=res[:, m, :], in0=y[:, m % 2, :], scalar=gate[:, 0:1], in1=res[:, m, :],
                                               op0=ALU.mult, op1=ALU.add).then_inc(added, 1)

            def iteration(i, has_next):
                if has_next:
                    layernorm_stats(i + 1)
                for k in range(K):
                    square_k(i, k)
                if has_next:
                    mix_tokens(i + 1, "k", 0)
                    for k in range(1, K):
                        mix_tokens(i + 1, "k", k)
                        low_part_mix(i + 1, "k", k - 1)
                    low_part_mix(i + 1, "k", K - 1)
                    mix_tokens(i + 1, "r", 0)
                    for k in range(1, K):
                        mix_tokens(i + 1, "r", k)
                        low_part_mix(i + 1, "r", k - 1)
                        combine(i, k - 1)
                    low_part_mix(i + 1, "r", K - 1)
                    combine(i, K - 1)
                else:
                    for m in range(T):
                        combine(i, m)

            nc.vector.memset(xT[:, :, 0:1], 0.0).then_inc(zeroed, 1)
            layernorm_stats(0)
            for n, name in enumerate("krv"):
                dve.wait_ge(w_high, n + 1)
                nc.vector.tensor_tensor(w[name][1][:], w_raw[name][:], w[name][0][:].bitcast(F32),
                                        ALU.subtract).then_inc(w_low, 1)
            dve.wait_ge(small_loaded, 16 * 3)
            dve.wait_ge(zeroed, 1)
            for n in "kr":
                for k in range(K):
                    mix_tokens(0, n, k)
                    low_part_mix(0, n, k)
            dve.wait_ge(gate_ready, 1)
            nc.vector.tensor_scalar(gate[:, 0:1], gate[:, 1:2], 0.5, None, ALU.mult).then_inc(zeroed, 1)
            dve.wait_ge(zeroed, 2)
            iteration(0, True)
            with dve.Fori(1, B - 1) as i:
                iteration(i, True)
            iteration(B - 1, False)

        @block.tensor
        def _(pe):
            def transpose_x(b, m):
                pe.wait_ge(ln_applied, T * b + m + 1)
                wait(pe, xt_copied, T * b + m - 1)
                for k in range(K):
                    last = nc.tensor.transpose(x_ps[m % 2][:, P * k:P * k + P], x_in[:, m, P * k:P * k + P], ident[:])
                last.then_inc(xt_done, 1)

            def project_k(b, g):
                if g == 0:
                    pe.wait_ge(mix_low["k"], K * (b + 1))
                wait(pe, square_done, K * b + g - 1)
                exact_product(nc, k_ps[g % 2][:], lambda k: [part[:, k, P * g:P * g + P] for part in w["k"]],
                              lambda k: [part[:, k, :] for part in mix["k"]], range(K)).then_inc(k_done, 1)

            def project_r(b, m):
                if m == 0:
                    pe.wait_ge(mix_low["r"], K * (b + 1))
                wait(pe, r_ready, T * b + m - 1)
                exact_product(nc, r_ps[m % 2][:], lambda k: [part[:, k, P * m:P * m + P] for part in mix["r"]],
                              lambda k: [part[:, k, :] for part in w["r"]], range(K)).then_inc(r_done, 1)

            def project_v(b, m):
                if m == 0:
                    pe.wait_ge(kact_low, K * (b + 1))
                wait(pe, y_done, T * b + m - 1)
                exact_product(nc, v_ps[m % 2][:], lambda k: [part[:, k, P * m:P * m + P] for part in kact],
                              lambda k: [part[:, k, :] for part in w["v"]], range(K)).then_inc(v_done, 1)

            def iteration(i, has_next):
                for g in range(K):
                    project_k(i, g)
                if has_next:
                    for m in range(T):
                        transpose_x(i + 1, m)
                for m in range(T):
                    project_r(i, m)
                for m in range(T):
                    project_v(i, m)

            pe.wait_ge(pool_const, 2)
            for m in range(T):
                transpose_x(0, m)
            pe.wait_ge(w_low, 3)
            iteration(0, True)
            with pe.Fori(1, B - 1) as i:
                iteration(i, True)
            iteration(B - 1, False)


def build(nc, x, ctxT, mask, g_xattn, g_ffn, wqT, bq, wkT, bk, wvT, bv, woT, bo, w_rT, w_kT, w_vT, mu_r, mu_k, out):
    x1 = nc.dram_tensor("x1", list(x.shape), F32, kind="Internal").ap()
    attention_phase(nc, x, ctxT, mask, g_xattn, wqT, bq, wkT, bk, wvT, bv, woT, bo, x1)
    channel_mix_phase(nc, x1, g_ffn, w_rT, w_kT, w_vT, mu_r, mu_k, out)


def lay_out(inputs):
    a = {n: np.asarray(v) for n, v in inputs.items()}
    D = a["x"].shape[-1]
    K, DH = D // P, D // HEADS

    def tiles(w):
        return np.ascontiguousarray(w.T.reshape(K, P, -1).transpose(1, 0, 2))

    def head_interleaved(v):
        return v.reshape(K, P // DH, DH, -1).swapaxes(1, 2).reshape(D, -1)

    def columns(v):
        return np.ascontiguousarray(v.reshape(K, P).T)

    return {
        "x": np.ascontiguousarray(a["x"]),
        "ctxT": np.ascontiguousarray(a["ctx_1024"].transpose(0, 2, 1)),
        "mask": np.ascontiguousarray(a["mask_BxS2_if1"]),
        "g_xattn": np.ascontiguousarray(a["g_xattn"]),
        "g_ffn": np.ascontiguousarray(a["g_ffn"]),
        "wqT": tiles(head_interleaved(a["L0_xattn_Wq"])),
        "bq": columns(head_interleaved(a["L0_xattn_bq"])),
        "wkT": tiles(head_interleaved(a["L0_xattn_Wk"])),
        "bk": columns(head_interleaved(a["L0_xattn_bk"])),
        "wvT": tiles(a["L0_xattn_Wv"]),
        "bv": columns(a["L0_xattn_bv"]),
        "woT": tiles(a["L0_xattn_Wo"]),
        "bo": np.ascontiguousarray(a["L0_xattn_bo"]),
        "w_rT": tiles(a["L0_ffn_W_r"]),
        "w_kT": tiles(a["L0_ffn_W_k"]),
        "w_vT": tiles(a["L0_ffn_W_v"]),
        "mu_r": columns(a["L0_ffn_mu_r"]),
        "mu_k": columns(a["L0_ffn_mu_k"]),
    }


def kernel(**inputs):
    import concourse.bacc as bacc
    from concourse.bass_utils import run_bass_kernel_spmd

    arrays = lay_out(inputs)
    nc = bacc.Bacc("TRN2", target_bir_lowering=False, num_devices=1)
    args = {n: nc.dram_tensor(f"in_{n}", v.shape, mybir.dt.from_np(v.dtype), kind="ExternalInput").ap()
            for n, v in arrays.items()}
    out = nc.dram_tensor("out_x", arrays["x"].shape, F32, kind="ExternalOutput").ap()
    build(nc, **args, out=out)
    run = run_bass_kernel_spmd(nc, [{f"in_{n}": v for n, v in arrays.items()}], core_ids=[0])
    return run.results[0]["out_x"]
```

```python
from contextlib import ExitStack

import numpy as np

import concourse.bass as bass
from concourse import mybir

ALU = mybir.AluOpType
ACT = mybir.ActivationFunctionType
F32 = mybir.dt.float32
F32R = mybir.dt.float32r
I32 = mybir.dt.int32

P = 128
HEADS = 16
LN_EPS = 1e-5
MASKED = -1e30
RSQRT_SEED = float(0x5F3759DF)
LN_STEPS = 14


def wait(engine, semaphore, count):
    if not isinstance(count, int) or count > 0:
        engine.wait_ge(semaphore, count)


def stand_alone(engine, semaphore, b):
    if not isinstance(b, int):
        engine.sem_inc(semaphore, 1)


def shared_room(nc, ctx, name, shape):
    with nc.sbuf_tensor(f"{name}_room", shape, F32) as room:
        pass
    return ctx.enter_context(nc.sbuf_tensor(name, shape, F32R)), room


def exact_product(nc, out, stationary, moving, steps, first=True, last=True):
    for n in steps:
        (s_high, s_low), (m_high, m_low) = stationary(n), moving(n)
        nc.tensor.matmul(out, s_high, m_high, start=first and n == steps[0], stop=False)
        nc.tensor.matmul(out, s_high, m_low, start=False, stop=False)
        done = nc.tensor.matmul(out, s_low, m_high, start=False, stop=last and n == steps[-1])
    return done


def invert_deviation(nc, pool, b, variances, newton, step, turns):
    at = LN_STEPS * b
    power, guess, variance = (newton[:, n, :] for n in range(3))
    stand_alone(pool, turns, b)
    nc.gpsimd.tensor_scalar(variance, variances, LN_EPS, None, ALU.add).then_inc(step, 1)
    pool.wait_ge(step, at + 1)
    stand_alone(pool, turns, b)
    nc.gpsimd.tensor_scalar(guess.bitcast(I32), variance.bitcast(I32), -0.5, RSQRT_SEED, ALU.mult,
                            ALU.add).then_inc(step, 1)
    pool.wait_ge(step, at + 2)
    for n in range(3):
        nc.gpsimd.tensor_tensor(power, guess, guess, ALU.mult).then_inc(step, 1)
        pool.wait_ge(step, at + 3 + 4 * n)
        nc.gpsimd.tensor_tensor(power, power, variance, ALU.mult).then_inc(step, 1)
        pool.wait_ge(step, at + 4 + 4 * n)
        stand_alone(pool, turns, b)
        nc.gpsimd.tensor_scalar(power, power, -0.5, 1.5, ALU.mult, ALU.add).then_inc(step, 1)
        pool.wait_ge(step, at + 5 + 4 * n)
        nc.gpsimd.tensor_tensor(guess, guess, power, ALU.mult).then_inc(step, 1)
        pool.wait_ge(step, at + 6 + 4 * n)


def attention_phase(nc, lent, x, ctxT, mask, g_xattn, wqT, bq, wkT, bk, wvT, bv, woT, bo, x1, ffn_wT):
    B, S, D = x.shape
    H = HEADS
    DH = D // H
    SCALE = float(DH) ** -0.5
    T = S // P
    K = D // P
    HG = P // DH
    PARTS = P // DH
    assert T == 4 and K == 4 and HG == 4 and PARTS == 4

    SEG = [P * t * (t + 1) // 2 for t in range(T + 1)]
    PT_AT = {0: 0, 1: 512, 3: 896, 2: 1024}
    PT_SETS = [[0], [1, 3], [2]]
    PT_COLS = [(0, 512), (512, 1024), (1024, 1280)]

    with ExitStack() as ctx:
        def sb(name, shape, dt=F32):
            return ctx.enter_context(nc.sbuf_tensor(name, shape, dt))

        def psum(name):
            return ctx.enter_context(nc.psum_tensor(name, [P, 512], F32))

        def sem(name):
            return ctx.enter_context(nc.semaphore(name))

        w = {"q": lent["wq"], "k": lent["wk"], "v": lent["wv"]}
        w["o"] = [sb(f"wo_{part}", [P, K, D], F32R) for part in ("high", "low")]
        xT, cT, ident = lent["xT"], lent["cT"], lent["ident"]
        x_io = [sb(f"x_io{n}", [P, D]) for n in range(2)]
        tile_in = [sb(f"tile_in{n}", [P, S]) for n in range(2)]
        staged = [sb(f"staged_{part}", [P, S], F32R) for part in ("high", "low")]
        q_stack = [sb(f"q_stack{n}", [P, HG, S], F32R) for n in range(2)]
        k_stack = [sb(f"k_stack{n}", [P, HG, S], F32R) for n in range(2)]
        v = sb("v", [P, T, D])
        probs = sb("probs", [P, 2, SEG[T]])
        probsT = sb("probsT", [P, HG, SEG[T]])
        bias = sb("bias", [P, SEG[T]])
        mask_row = sb("mask_row", [P, S])
        attn, attn_room = zip(*(shared_room(nc, ctx, f"attn_{part}", [P, K, S]) for part in ("high", "low")))
        norm = sb("norm", [P, S])
        bo_gated = sb("bo_gated", [P, D])
        causal = sb("causal", [P, P])
        columns = sb("columns", [P, 3, K])
        gate = sb("gate", [P, 1])
        least = sb("least", [P, K, T, HG])
        sums = sb("sums", [P, K, T, HG])
        live = sb("live", [P, T, HG])
        inverse = sb("inverse", [P, T, HG])
        stats = sb("stats", [P, T, 6])
        moments = sb("moments", [P, T, 2])
        newton = sb("newton", [P, 3, T])

        score_ps = [psum(f"score_ps{n}") for n in range(2)]
        pt_ps = [psum(f"pt_ps{n}") for n in range(2)]
        proj_ps = [psum(f"proj_ps{n}") for n in range(2)]
        value_ps = psum("value_ps")
        norm_ps = psum("norm_ps")

        w_loaded = {n: sem(f"w{n}_loaded") for n in "qkvo"}
        sp_turns, pool_turns, dve_turns = sem("sp_turns"), sem("pool_turns"), sem("dve_turns")
        ffn_loaded = {n: sem(f"ffn_w{n}_loaded") for n in "krv"}
        ffn_high, ffn_low, ffn_x_loaded = sem("ffn_w_high"), sem("ffn_w_low"), sem("ffn_x_first_loaded")
        w_high = sem("w_high")
        w_low = sem("w_low")
        small_loaded = sem("small_loaded")
        pool_const = sem("pool_const")
        gate_ready = sem("gate_ready")
        x_peeked = [sem(f"x_peeked{n}") for n in range(2)]
        x_loaded = [sem(f"x_loaded{m}") for m in range(T)]
        bn_done = sem("bn_done")
        ln_step = sem("ln_step")
        ln_stats = sem("ln_stats")
        ln_applied = sem("ln_applied")
        xt_done = sem("xt_done")
        xt_high = sem("xt_high")
        xt_low = sem("xt_low")
        c_raw_loaded = sem("c_raw_loaded")
        c_loaded = [sem(f"c_loaded{n}") for n in range(2)]
        c_high = sem("c_high")
        c_low = sem("c_low")
        q_done, k_done, v_done, o_done = (sem(f"{n}_done") for n in "qkvo")
        q_high, k_high = sem("q_high"), sem("k_high")
        q_low, k_low = sem("q_low"), sem("k_low")
        v_copied = sem("v_copied")
        q_stacked = [sem(f"q_stacked{n}") for n in range(2)]
        k_stacked = [sem(f"k_stacked{n}") for n in range(2)]
        mask_loaded = sem("mask_loaded")
        mask_ready = sem("mask_ready")
        bias_ready = sem("bias_ready")
        scores_done = sem("scores_done")
        scores_read = sem("scores_read")
        exp_done = sem("exp_done")
        pt_done = sem("pt_done")
        pt_act = sem("pt_act")
        pt_dve = sem("pt_dve")
        values_done = sem("values_done")
        inv_step = sem("inv_step")
        norm_spread = sem("norm_spread")
        norm_done = sem("norm_done")
        norm_copied = sem("norm_copied")
        normalised = sem("normalised")
        attn_high = sem("attn_high")
        attn_low = sem("attn_low")
        res_loaded = [sem(f"res_loaded{n}") for n in range(2)]
        res_ready = sem("res_ready")
        o_added = sem("o_added")
        x1_stored = [sem(f"x1_stored{n}") for n in range(2)]

        def room(tensor, n):
            flat = tensor[:].rearrange("p a b -> p (a b)")[:, K * D * n:K * D * (n + 1)]
            return flat.rearrange("p (k n) -> p k n", k=K)

        c_raw = room(probs, 0)
        w_raw = {"q": room(probsT, 0), "k": room(probsT, 1), "v": attn_room[0][:], "o": attn_room[1][:]}

        ffn_raw = {"k": lent["wq_room"][0], "r": lent["wq_room"][1], "v": lent["wk_room"][0]}
        ffn_w = {"k": xT, "r": cT, "v": w["v"]}
        ffn_x = lent["wk_room"][1]

        SETS = 3 * H
        TILES = T * H
        STATS_ORDER = (2, 3, 0, 1)
        BANK = {"v": (0, 1, 0, 1), "q": (0, 0, 0, 0), "o": (1, 1, 0, 1), "k": (1, 1, 0, 0), "x": (1, 1, 0, 1)}

        def proj(kind, n):
            return proj_ps[BANK[kind][n]]

        block = ctx.enter_context(nc.Block())

        def x_tile(m):
            return tile_in[m] if m < 2 else x_io[m - 2]

        def stacked_count(b, g):
            return 64 * (K // 2) * b + 64 * (g // 2 + 1)

        @block.sync
        def _(sp):
            def peek_x(b, n):
                sp.wait_ge(c_low, K * b)
                stand_alone(sp, sp_turns, b)
                sp.dma_start(tile_in[n][:], x[b, P * (n + 2):P * (n + 3)]).then_inc(x_peeked[n], 16)

            def load_x(b, m):
                if m >= 2:
                    wait(sp, x1_stored[m % 2], 32 * (b - 1))
                    wait(sp, xt_done, T * b)
                elif not isinstance(b, int) or b > 0:
                    sp.wait_ge(bn_done, T * b + m + 1)
                stand_alone(sp, sp_turns, b)
                sp.dma_start(x_tile(m)[:], x[b, P * m:P * m + P]).then_inc(x_loaded[m], 16)

            def load_c(b, k):
                if k < 2:
                    sp.wait_ge(xt_done, T * b + k + 1)
                else:
                    sp.wait_ge(c_low, K * b + k - 1)
                stand_alone(sp, sp_turns, b)
                sp.dma_start(tile_in[k % 2][:], ctxT[b, P * k:P * k + P]).then_inc(c_loaded[k % 2], 16)

            def load_mask(b):
                wait(sp, bias_ready, 7 * b)
                stand_alone(sp, sp_turns, b)
                sp.dma_start(mask_row[:].bitcast(I32), mask[b].partition_broadcast(P)).then_inc(mask_loaded, 16)

            def stack(b, g, low_done, stacks, parts, stacked):
                sp.wait_ge(low_done, K * b + g + 1)
                stand_alone(sp, sp_turns, b)
                wait(sp, scores_done, SETS * b + 3 * HG * (g - 1))
                for p in range(PARTS):
                    sp.dma_start(stacks[g % 2][DH * p:DH * p + DH, :, :].bitcast(F32),
                                 staged[parts[p]][:].bitcast(F32)).then_inc(stacked[g % 2], 16)

            def stack_q(b, g):
                stack(b, g, q_low, q_stack, (0, 0, 1, 1), q_stacked)

            def stack_k(b, g):
                stack(b, g, k_low, k_stack, (0, 1, 0, 1), k_stacked)

            def load_residual(b, m, last):
                if m >= 2 or last:
                    sp.wait_ge(x1_stored[m % 2], 32 * b + (16 if m >= 2 else 0))
                else:
                    sp.wait_ge(xt_done, T * (b + 1) + m + 3)
                stand_alone(sp, sp_turns, b)
                sp.dma_start(x_io[m % 2][:], x[b, P * m:P * m + P]).then_inc(res_loaded[m % 2], 16)

            def store_x1(b, m):
                sp.wait_ge(o_added, T * b + m + 1)
                stand_alone(sp, sp_turns, b)
                sp.dma_start(x1[b, P * m:P * m + P], x_io[m % 2][:]).then_inc(x1_stored[m % 2], 16)

            def load_ffn():
                sp.wait_ge(q_done, K * B)
                for n in "kr":
                    sp.dma_start(ffn_raw[n][:], ffn_wT[n]).then_inc(ffn_loaded[n], 16)
                sp.wait_ge(k_done, K * B)
                sp.dma_start(ffn_raw["v"][:], ffn_wT["v"]).then_inc(ffn_loaded["v"], 16)
                for n in range(2):
                    sp.wait_ge(x1_stored[n], 32)
                sp.dma_start(ffn_x[:], x1[0].rearrange("(t p) d -> p t d", p=P)).then_inc(ffn_x_loaded, 16)

            def iteration(i, has_prev, has_next):
                if has_next:
                    peek_x(i + 1, 0)
                    peek_x(i + 1, 1)
                stack_k(i, 1)
                if has_prev:
                    load_residual(i - 1, 0, not has_next)
                    load_residual(i - 1, 1, not has_next)
                if has_next:
                    load_mask(i + 1)
                    load_x(i + 1, 0)
                    load_x(i + 1, 1)
                stack_q(i, 2)
                if has_prev:
                    store_x1(i - 1, 0)
                    load_residual(i - 1, 2, False)
                stack_k(i, 2)
                if has_prev:
                    store_x1(i - 1, 1)
                    load_residual(i - 1, 3, False)
                    store_x1(i - 1, 2)
                if has_next:
                    load_x(i + 1, 2)
                if has_prev:
                    store_x1(i - 1, 3)
                if has_next:
                    load_c(i + 1, 0)
                    load_x(i + 1, 3)
                stack_q(i, 3)
                if has_next:
                    load_c(i + 1, 1)
                stack_k(i, 3)
                if has_next:
                    load_c(i + 1, 2)
                    load_c(i + 1, 3)
                    stack_q(i + 1, 0)
                    stack_k(i + 1, 0)
                    stack_q(i + 1, 1)
                else:
                    load_ffn()

            for m in range(T):
                load_x(0, m)
            sp.dma_start(w_raw["q"], wqT).then_inc(w_loaded["q"], 16)
            sp.dma_start(c_raw, ctxT[0].rearrange("(k p) s -> p k s", p=P)).then_inc(c_raw_loaded, 16)
            sp.dma_start(w_raw["k"], wkT).then_inc(w_loaded["k"], 16)
            for n, col in enumerate((bq, bk, bv)):
                sp.dma_start(columns[:, n, :], col).then_inc(small_loaded, 16)
            sp.dma_start(gate[:], g_xattn.partition_broadcast(P)).then_inc(small_loaded, 16)
            sp.dma_start(bo_gated[:], bo.partition_broadcast(P)).then_inc(small_loaded, 16)
            load_mask(0)
            sp.dma_start(w_raw["v"], wvT).then_inc(w_loaded["v"], 16)
            sp.dma_start(w_raw["o"], woT).then_inc(w_loaded["o"], 16)
            stack_q(0, 0)
            stack_k(0, 0)
            stack_q(0, 1)
            iteration(0, False, True)
            with sp.Fori(1, B - 1) as i:
                iteration(i, True, True)
            iteration(B - 1, True, False)
            for m in range(2):
                load_residual(B - 1, m, True)
            for m in range(T):
                store_x1(B - 1, m)
                if m < 2:
                    load_residual(B - 1, m + 2, True)
            for n in range(2):
                sp.wait_ge(x1_stored[n], 32 * B)
            sp.wait_ge(ffn_x_loaded, 16)


        @block.gpsimd
        def _(pool):
            def spread_inverse(b, t):
                pool.wait_ge(inv_step, 2 * (K * b + t + 1))
                wait(pool, attn_low, K * b + t)
                stand_alone(pool, pool_turns, b)
                nc.gpsimd.tensor_copy(norm[:].rearrange("p (h d) -> p h d", d=DH),
                                      inverse[:].rearrange("p t h -> p (t h)").unsqueeze(2).broadcast_to([P, T * HG, DH])
                                      ).then_inc(norm_spread, 1)

            def mask_to_bias(b):
                pool.wait_ge(mask_loaded, 16 * (b + 1))
                stand_alone(pool, pool_turns, b)
                nc.gpsimd.tensor_scalar(mask_row[:], mask_row[:].bitcast(I32), 0, MASKED, ALU.is_equal,
                                        ALU.mult).then_inc(mask_ready, 1)

            def add_residual_bias(b, m):
                pool.wait_ge(res_loaded[m % 2], 16 * (T // 2 * b + m // 2 + 1))
                nc.gpsimd.tensor_tensor(x_io[m % 2][:], x_io[m % 2][:], bo_gated[:], ALU.add).then_inc(res_ready, 1)

            def invert_deviations(b):
                pool.wait_ge(ln_stats, T * (b + 1))
                wait(pool, ln_applied, T * b)
                invert_deviation(nc, pool, b, moments[:, :, 1], newton, ln_step, pool_turns)

            def apply_layernorm(b, m):
                pool.wait_ge(x_loaded[m], 16 * (b + 1))
                stand_alone(pool, pool_turns, b)
                nc.gpsimd.tensor_scalar(x_tile(m)[:], x_tile(m)[:], moments[:, m, 0:1], newton[:, 1, m:m + 1],
                                        ALU.subtract, ALU.mult).then_inc(ln_applied, 1)

            def split_c(b, k):
                pool.wait_ge(c_loaded[k % 2], 16 * (K // 2 * (b - 1) + k // 2 + 1))
                wait(pool, k_done, K * b)
                stand_alone(pool, pool_turns, b)
                nc.gpsimd.tensor_copy(cT[0][:, k, :], tile_in[k % 2][:]).then_inc(c_high, 1)
                pool.wait_ge(c_high, K * b + k + 1)
                nc.gpsimd.tensor_tensor(cT[1][:, k, :], tile_in[k % 2][:], cT[0][:, k, :].bitcast(F32),
                                        ALU.subtract).then_inc(c_low, 1)

            def iteration(i, has_prev, has_next):
                if has_prev:
                    spread_inverse(i - 1, 3)
                    add_residual_bias(i - 1, 0)
                    add_residual_bias(i - 1, 1)
                if has_next:
                    mask_to_bias(i + 1)
                spread_inverse(i, 0)
                if has_next:
                    invert_deviations(i + 1)
                if has_prev:
                    add_residual_bias(i - 1, 2)
                if has_next:
                    apply_layernorm(i + 1, 0)
                if has_prev:
                    add_residual_bias(i - 1, 3)
                if has_next:
                    apply_layernorm(i + 1, 1)
                spread_inverse(i, 1)
                if has_next:
                    apply_layernorm(i + 1, 2)
                    split_c(i + 1, 0)
                    apply_layernorm(i + 1, 3)
                    for k in range(1, K):
                        split_c(i + 1, k)
                spread_inverse(i, 2)

            nc.gpsimd.memset(ident[:], 0.0).then_inc(pool_const, 1)
            nc.gpsimd.memset(causal[:], 0.0).then_inc(pool_const, 1)
            pool.wait_ge(pool_const, 2)
            nc.gpsimd.affine_select(out=ident[:], in_=ident[:], compare_op=ALU.not_equal, fill=1.0, base=0,
                                    pattern=[[-1, P]], channel_multiplier=1).then_inc(pool_const, 1)
            nc.gpsimd.affine_select(out=causal[:], in_=causal[:], compare_op=ALU.is_ge, fill=MASKED, base=0,
                                    pattern=[[-1, P]], channel_multiplier=1).then_inc(pool_const, 1)
            invert_deviations(0)
            mask_to_bias(0)
            pool.wait_ge(gate_ready, 1)
            nc.gpsimd.tensor_scalar(bo_gated[:], bo_gated[:], gate[:, 0:1], None, ALU.mult).then_inc(pool_const, 1)
            pool.wait_ge(pool_const, 5)
            iteration(0, False, True)
            with pool.Fori(1, B - 1) as i:
                iteration(i, True, True)
            iteration(B - 1, True, False)
            spread_inverse(B - 1, 3)
            invert_deviations(B)
            for m in range(T):
                add_residual_bias(B - 1, m)

        @block.scalar
        def _(act):
            def high_part_x(b, m):
                act.wait_ge(xt_done, T * b + m + 1)
                wait(act, q_done, K * b)
                nc.scalar.copy(xT[0][:, :, P * m:P * m + P], proj("x", m)[:].rearrange("p (k n) -> p k n", k=K)
                               ).then_inc(xt_high, 1)

            def high_part_q(b, g):
                act.wait_ge(q_done, K * b + g + 1)
                if g > 0:
                    act.wait_ge(k_stacked[(g - 1) % 2], stacked_count(b, g - 1))
                else:
                    wait(act, k_stacked[1], 64 * (K // 2) * b)
                nc.scalar.activation(staged[0][:], proj("q", g)[:], ACT.Identity, bias=columns[:, 0, g:g + 1]
                                     ).then_inc(q_high, 1)

            def high_part_k(b, g):
                act.wait_ge(k_done, K * b + g + 1)
                act.wait_ge(q_stacked[g % 2], stacked_count(b, g))
                nc.scalar.activation(staged[0][:], proj("k", g)[:], ACT.Identity, bias=columns[:, 1, g:g + 1]
                                     ).then_inc(k_high, 1)

            def copy_v(b, m):
                act.wait_ge(v_done, T * b + m + 1)
                wait(act, values_done, K * b)
                nc.scalar.copy(v[:, m, :], proj("v", m)[:]).then_inc(v_copied, 1)

            def copy_norm(b, t):
                act.wait_ge(norm_done, K * b + t + 1)
                nc.scalar.copy(norm[:], norm_ps[:]).then_inc(norm_copied, 1)

            def high_part_attn(b, t):
                act.wait_ge(normalised, K * b + t + 1)
                if t == 0:
                    wait(act, o_done, T * b)
                nc.scalar.activation(attn[0][:, t, :], norm[:], ACT.Identity, bias=columns[:, 2, t:t + 1]
                                     ).then_inc(attn_high, 1)

            def transposed(b, h, n):
                act.wait_ge(pt_done, SETS * b + 3 * h + n + 1)
                wait(act, values_done, K * b + h // HG)
                lo, hi = PT_COLS[n]
                nc.scalar.copy(probsT[:, h % HG, lo:hi], pt_ps[n % 2][:, 0:hi - lo]).then_inc(pt_act, 1)

            def exponent(b, h, t):
                act.wait_ge(scores_read, TILES * b + T * h + t + 1)
                here = probs[:, h % 2, SEG[t]:SEG[t + 1]]
                at = (h // HG, t, h % HG)
                nc.scalar.activation(here, here, ACT.Exp, bias=least[:, at[0], at[1], at[2]:at[2] + 1], scale=-1.0,
                                     accum_out=sums[:, at[0], at[1], at[2]:at[2] + 1]).then_inc(exp_done, 1)

            def split_ffn(name):
                act.wait_ge(ffn_loaded[name], 16)
                act.wait_ge({"k": q_done, "r": k_done, "v": v_done}[name], K * B)
                nc.scalar.copy(ffn_w[name][0][:], ffn_raw[name][:]).then_inc(ffn_high, 1)

            def after(i, s, has_prev, has_next):
                if s == 0:
                    high_part_k(i, 1)
                    copy_v(i, 0)
                if s == 1:
                    copy_v(i, 1)
                    if has_prev:
                        high_part_attn(i - 1, 3)
                    copy_v(i, 2)
                if s == 2:
                    copy_v(i, 3)
                    high_part_q(i, 2)
                if s == 4:
                    high_part_k(i, 2)
                if s == 7:
                    high_part_attn(i, 0)
                if s == 8:
                    high_part_q(i, 3)
                if s == 9:
                    high_part_k(i, 3)
                if 8 <= s <= 10 and has_next:
                    high_part_x(i + 1, s - 8)
                if s == 10 and has_next:
                    high_part_x(i + 1, 3)
                if s == 10:
                    high_part_attn(i, 1)
                if 11 <= s <= 13 and not has_next:
                    split_ffn("krv"[s - 11])
                if s == 12 and has_next:
                    high_part_q(i + 1, 0)
                if s == 13 and has_next:
                    high_part_k(i + 1, 0)
                if s == 14:
                    high_part_attn(i, 2)
                    if has_next:
                        high_part_q(i + 1, 1)

            def iteration(i, has_prev, has_next):
                for s in range(H):
                    before = (i, s - 1) if s > 0 else (i - 1, H - 1)
                    exponent(i, s, 0)
                    exponent(i, s, 1)
                    if s > 0 or has_prev:
                        transposed(*before, 0)
                    if s % HG == 1 and (s > 1 or has_prev):
                        copy_norm(*((i, s // HG - 1) if s > 1 else (i - 1, K - 1)))
                    exponent(i, s, 2)
                    exponent(i, s, 3)
                    if s > 0 or has_prev:
                        transposed(*before, 2)
                    after(i, s, has_prev, has_next)

            def split_weights(n, name):
                act.wait_ge(w_loaded[name], 16)
                nc.scalar.copy(w[name][0][:], w_raw[name]).then_inc(w_high, 1)

            split_weights(0, "q")
            act.wait_ge(c_raw_loaded, 16)
            nc.scalar.copy(cT[0][:], c_raw).then_inc(c_high, K)
            for m in range(T):
                high_part_x(0, m)
            split_weights(1, "k")
            act.wait_ge(small_loaded, 16 * 5)
            high_part_q(0, 0)
            high_part_k(0, 0)
            split_weights(2, "v")
            high_part_q(0, 1)
            nc.scalar.activation(gate[:], gate[:], ACT.Tanh).then_inc(gate_ready, 1)
            split_weights(3, "o")
            iteration(0, False, True)
            with act.Fori(1, B - 1) as i:
                iteration(i, True, True)
            iteration(B - 1, True, False)
            for n in (0, 2):
                transposed(B - 1, H - 1, n)
            copy_norm(B - 1, 3)
            high_part_attn(B - 1, 3)

        @block.vector
        def _(dve):
            def layernorm_stats(b, n):
                m = STATS_ORDER[n]
                if m < 2 or isinstance(b, int) and b == 0:
                    dve.wait_ge(x_loaded[m], 16 * (b + 1))
                    tile = x_tile(m)
                else:
                    dve.wait_ge(x_peeked[m - 2], 16 * b)
                    tile = tile_in[m - 2]
                wait(dve, ln_stats, T * b)
                nc.vector.bn_stats(stats[:, m, :], tile[:]).then_inc(bn_done, 1)

            def aggregate_stats(b):
                dve.wait_ge(bn_done, T * (b + 1))
                wait(dve, ln_applied, T * b)
                stand_alone(dve, dve_turns, b)
                for m in range(T):
                    nc.vector.bn_aggr(moments[:, m, :], stats[:, m, :]).then_inc(ln_stats, 1)

            def normalise_x(m, tile):
                nc.vector.tensor_scalar(tile, tile, moments[:, m, 0:1], newton[:, 1, m:m + 1], ALU.subtract,
                                        ALU.mult).then_inc(ln_applied, 1)

            def low_part_x(b, m):
                dve.wait_ge(xt_high, T * b + m + 1)
                nc.vector.tensor_tensor(xT[1][:, :, P * m:P * m + P], proj("x", m)[:].rearrange("p (k n) -> p k n", k=K),
                                        xT[0][:, :, P * m:P * m + P].bitcast(F32), ALU.subtract).then_inc(xt_low, 1)

            def low_part_q(b, g):
                dve.wait_ge(q_high, K * b + g + 1)
                nc.vector.scalar_tensor_tensor(out=staged[1][:], in0=proj("q", g)[:], scalar=columns[:, 0, g:g + 1],
                                               in1=staged[0][:].bitcast(F32), op0=ALU.add, op1=ALU.subtract
                                               ).then_inc(q_low, 1)

            def low_part_k(b, g):
                dve.wait_ge(k_high, K * b + g + 1)
                nc.vector.scalar_tensor_tensor(out=staged[1][:], in0=proj("k", g)[:], scalar=columns[:, 1, g:g + 1],
                                               in1=staged[0][:].bitcast(F32), op0=ALU.add, op1=ALU.subtract
                                               ).then_inc(k_low, 1)

            def build_bias(b, t):
                dve.wait_ge(mask_ready, b + 1)
                wait(dve, scores_read, TILES * b - (T - 1 - t))
                nc.vector.tensor_tensor(bias[:, SEG[t + 1] - P:SEG[t + 1]], mask_row[:, P * t:P * t + P], causal[:],
                                        ALU.add).then_inc(bias_ready, 1)
                if t > 0:
                    nc.vector.tensor_copy(bias[:, SEG[t]:SEG[t + 1] - P], mask_row[:, 0:P * t]).then_inc(bias_ready, 1)

            def bias_scores(b, h, t):
                c = max(t - 1, 0)
                if h == 0:
                    dve.wait_ge(bias_ready, 7 * b + 2 * t + 1)
                if t != 1:
                    dve.wait_ge(scores_done, SETS * b + 3 * h + c + 1)
                    if t == 0:
                        wait(dve, pt_done, SETS * b + 3 * (h - 1))
                if t != 1 or h == 0:
                    stand_alone(dve, dve_turns, b)
                at = P if t == 1 else 0
                width = P * (t + 1)
                nc.vector.tensor_tensor_reduce(
                    out=probs[:, h % 2, SEG[t]:SEG[t + 1]], in0=score_ps[(h + c) % 2][:, at:at + width],
                    in1=bias[:, SEG[t]:SEG[t + 1]], scale=-SCALE, scalar=3e38, op0=ALU.add, op1=ALU.min,
                    accum_out=least[:, h // HG, t, h % HG:h % HG + 1]).then_inc(scores_read, 1)

            def transposed(b, h):
                dve.wait_ge(pt_done, SETS * b + 3 * h + 2)
                wait(dve, values_done, K * b + h // HG)
                lo, hi = PT_COLS[1]
                nc.vector.tensor_copy(probsT[:, h % HG, lo:hi], pt_ps[1][:, 0:hi - lo]).then_inc(pt_dve, 1)

            def invert_sums(b, t):
                dve.wait_ge(exp_done, TILES * b + T * HG * (t + 1))
                nc.vector.scalar_tensor_tensor(out=live[:], in0=least[:, t], scalar=-MASKED / 100, in1=sums[:, t],
                                               op0=ALU.is_lt, op1=ALU.mult).then_inc(inv_step, 1)
                dve.wait_ge(inv_step, 2 * (K * b + t) + 1)
                wait(dve, norm_spread, K * b + t)
                nc.vector.reciprocal(inverse[:], live[:]).then_inc(inv_step, 1)

            def normalise(b, t):
                dve.wait_ge(norm_copied, K * b + t + 1)
                dve.wait_ge(values_done, K * b + t + 1)
                nc.vector.tensor_tensor(norm[:], value_ps[:], norm[:], ALU.mult).then_inc(normalised, 1)

            def low_part_attn(b, t):
                dve.wait_ge(attn_high, K * b + t + 1)
                nc.vector.scalar_tensor_tensor(out=attn[1][:, t, :], in0=norm[:], scalar=columns[:, 2, t:t + 1],
                                               in1=attn[0][:, t, :].bitcast(F32), op0=ALU.add, op1=ALU.subtract
                                               ).then_inc(attn_low, 1)

            def add_output(b, m):
                dve.wait_ge(o_done, T * b + m + 1)
                dve.wait_ge(res_ready, T * b + m + 1)
                nc.vector.scalar_tensor_tensor(out=x_io[m % 2][:], in0=proj("o", m)[:], scalar=gate[:, 0:1],
                                               in1=x_io[m % 2][:], op0=ALU.mult, op1=ALU.add).then_inc(o_added, 1)

            def split_ffn(n, name):
                dve.wait_ge(ffn_high, n + 1)
                nc.vector.tensor_tensor(ffn_w[name][1][:], ffn_raw[name][:],
                                        ffn_w[name][0][:].bitcast(F32), ALU.subtract).then_inc(ffn_low, 1)

            def between(i, s, has_prev, has_next):
                if s == 0 and has_prev:
                    invert_sums(i - 1, 3)
                if s == 1:
                    if has_prev:
                        normalise(i - 1, 3)
                if s == 2 and has_prev:
                    low_part_attn(i - 1, 3)
                if s == 3:
                    low_part_q(i, 2)
                if s == 4:
                    if has_prev:
                        add_output(i - 1, 0)
                    invert_sums(i, 0)
                if s == 5:
                    low_part_k(i, 2)
                if s == 6:
                    normalise(i, 0)
                    if has_prev:
                        add_output(i - 1, 1)
                if s == 7 and has_prev:
                    add_output(i - 1, 2)
                if s == 8:
                    if has_prev:
                        add_output(i - 1, 3)
                    low_part_attn(i, 0)
                    invert_sums(i, 1)
                if s == 10:
                    low_part_k(i, 3)
                if 9 <= s <= 11 and has_next:
                    low_part_x(i + 1, s - 9)
                if s == 11 and has_next:
                    low_part_x(i + 1, 3)
                if s == 10:
                    normalise(i, 1)
                if s == 11:
                    low_part_attn(i, 1)
                if s == 12:
                    invert_sums(i, 2)
                if s == 14:
                    normalise(i, 2)
                if s == 15:
                    low_part_attn(i, 2)
                    if has_next:
                        low_part_q(i + 1, 1)

            def split_weights(n, name):
                dve.wait_ge(w_high, n + 1)
                nc.vector.tensor_tensor(w[name][1][:], w_raw[name], w[name][0][:].bitcast(F32),
                                        ALU.subtract).then_inc(w_low, 1)

            def at_end(i, s, has_prev, has_next):
                if s == 0:
                    low_part_k(i, 1)
                if s < 4 and has_next:
                    layernorm_stats(i + 1, s)
                    if s == 3:
                        aggregate_stats(i + 1)
                if s == 2 and not has_prev:
                    split_weights(3, "o")
                if s == 8:
                    low_part_q(i, 3)
                if s == 12 and has_next:
                    low_part_q(i + 1, 0)
                if s == 13 and has_next:
                    low_part_k(i + 1, 0)
                if 12 <= s <= 14 and not has_next:
                    split_ffn(s - 12, "krv"[s - 12])

            def iteration(i, has_prev, has_next):
                for s in range(H):
                    rebuild = has_next and s == H - 1
                    for t in range(3):
                        bias_scores(i, s, t)
                        if rebuild and t > 0:
                            build_bias(i + 1, t - 1)
                    between(i, s, has_prev, has_next)
                    bias_scores(i, s, 3)
                    if rebuild:
                        build_bias(i + 1, 2)
                        build_bias(i + 1, 3)
                    if s > 0:
                        transposed(i, s - 1)
                    elif has_prev:
                        transposed(i - 1, H - 1)
                    at_end(i, s, has_prev, has_next)

            for n in range(T):
                layernorm_stats(0, n)
            aggregate_stats(0)
            split_weights(0, "q")
            dve.wait_ge(ln_step, LN_STEPS)
            for m in range(T):
                normalise_x(m, x_tile(m)[:])
            dve.wait_ge(c_high, K)
            nc.vector.tensor_tensor(cT[1][:], c_raw, cT[0][:].bitcast(F32), ALU.subtract).then_inc(c_low, K)
            for m in range(T):
                low_part_x(0, m)
            split_weights(1, "k")
            low_part_q(0, 0)
            low_part_k(0, 0)
            split_weights(2, "v")
            low_part_q(0, 1)
            dve.wait_ge(pool_const, 5)
            for t in range(T):
                build_bias(0, t)
            iteration(0, False, True)
            with dve.Fori(1, B - 1) as i:
                iteration(i, True, True)
            iteration(B - 1, True, False)
            transposed(B - 1, H - 1)
            invert_sums(B - 1, 3)
            dve.wait_ge(ffn_x_loaded, 16)
            for m in range(T):
                nc.vector.bn_stats(stats[:, m, :], ffn_x[:, m, :]).then_inc(bn_done, 1)
            aggregate_stats(B)
            normalise(B - 1, 3)
            low_part_attn(B - 1, 3)
            for m in range(T):
                add_output(B - 1, m)
                if m == 0:
                    dve.wait_ge(ln_step, LN_STEPS * (B + 1))
                normalise_x(m, ffn_x[:, m, :])

        @block.tensor
        def _(pe):
            def scores(b, h, c):
                g, j = h // HG, h % HG
                if j == 0 and c == 0:
                    pe.wait_ge(q_stacked[g % 2], stacked_count(b, g))
                    pe.wait_ge(k_stacked[g % 2], stacked_count(b, g))
                wait(pe, scores_read, TILES * b + T * h + (-1, 0, 2)[c])
                bank = score_ps[(h + c) % 2]
                for t in ((0, 1), (2,), (3,))[c]:
                    at = P if t == 1 else 0
                    last = nc.tensor.matmul(bank[:, at:at + P * (t + 1)], q_stack[g % 2][:, j, P * t:P * t + P],
                                            k_stack[g % 2][:, j, 0:P * (t + 1)], start=True, stop=True)
                last.then_inc(scores_done, 1)

            def transpose_probs(b, h, n):
                if n == 0:
                    pe.wait_ge(exp_done, TILES * b + T * (h + 1))
                if n == 1:
                    wait(pe, pt_dve, H * b + h)
                else:
                    wait(pe, pt_act, 2 * (H * b + h) + n // 2)
                for k in PT_SETS[n]:
                    for t in range(k, T):
                        at = PT_AT[k] - PT_COLS[n][0] + P * (t - k)
                        last = nc.tensor.transpose(pt_ps[n % 2][:, at:at + P],
                                                   probs[:, h % 2, SEG[t] + P * k:SEG[t] + P * k + P], ident[:])
                last.then_inc(pt_done, 1)

            def transpose_inverse(b, t):
                pe.wait_ge(norm_spread, K * b + t + 1)
                wait(pe, norm_copied, K * b + t)
                for n in range(T):
                    last = nc.tensor.transpose(norm_ps[:, P * n:P * n + P], norm[:, P * n:P * n + P], ident[:])
                last.then_inc(norm_done, 1)

            def values(b, t):
                pe.wait_ge(pt_act, 2 * H * b + 2 * HG * (t + 1))
                pe.wait_ge(pt_dve, H * b + HG * (t + 1))
                if t == 0:
                    pe.wait_ge(v_copied, T * (b + 1))
                wait(pe, normalised, K * b + t)
                for k in range(T):
                    for j in range(HG):
                        last = nc.tensor.matmul(value_ps[DH * j:DH * j + DH, P * k:S],
                                                v[:, k, P * t + DH * j:P * t + DH * j + DH],
                                                probsT[:, j, PT_AT[k]:PT_AT[k] + S - P * k],
                                                start=(k == 0), stop=(k == T - 1), skip_group_check=True)
                last.then_inc(values_done, 1)

            def product(kind, n, k, stationary, moving, done):
                last = exact_product(nc, proj(kind, n)[:], stationary, moving, [k], k == 0, k == K - 1)
                if k == K - 1:
                    last.then_inc(done, 1)

            def project_q(b, g, k, has_prev=True):
                if k == 0 and g == 0:
                    pe.wait_ge(xt_low, T * (b + 1))
                elif k == 0 and g == 1:
                    pe.wait_ge(q_low, K * b + 1)
                elif k == 0 and g == 2:
                    pe.wait_ge(v_copied, T * b + 3)
                elif k == 0 and has_prev:
                    pe.wait_ge(o_added, T * b - 1)
                elif k == 0:
                    pe.wait_ge(k_low, K * b + 3)
                product("q", g, k, lambda k: [part[:, k, P * g:P * g + P] for part in w["q"]],
                        lambda k: [part[:, k, :] for part in xT], q_done)

            def project_k(b, g, k):
                if k == 0 and g == 0:
                    pe.wait_ge(c_low, K * (b + 1))
                    pe.wait_ge(xt_low, T * (b + 1))
                elif k == 0 and g == 1:
                    pe.wait_ge(k_low, K * b + 1)
                elif k == 0:
                    pe.wait_ge(q_low, K * b + g + 1)
                product("k", g, k, lambda k: [part[:, k, P * g:P * g + P] for part in w["k"]],
                        lambda k: [part[:, k, :] for part in cT], k_done)

            def project_v(b, m, k):
                if k == 0 and m == 0:
                    pe.wait_ge(q_low, K * b + 2)
                elif k == 0 and m == 1:
                    pe.wait_ge(k_low, K * b + 2)
                elif k == 0:
                    pe.wait_ge(v_copied, T * b + m - 1)
                product("v", m, k, lambda k: [part[:, k, P * m:P * m + P] for part in cT],
                        lambda k: [part[:, k, :] for part in w["v"]], v_done)

            def project_o(b, m, k, has_next=True):
                if k == 0 and m == 0:
                    pe.wait_ge(attn_low, K * (b + 1))
                    if has_next:
                        pe.wait_ge(v_copied, T * (b + 2))
                elif k == 0 and m == 2 and has_next:
                    pe.wait_ge(k_low, K * (b + 1) + 3)
                elif k == 0 and m == 2:
                    pe.wait_ge(k_low, K * (b + 1))
                elif k == 0:
                    pe.wait_ge(o_added, T * b + (1 if m == 1 else 2))
                product("o", m, k, lambda k: [part[:, k, P * m:P * m + P] for part in attn],
                        lambda k: [part[:, k, :] for part in w["o"]], o_done)

            def transpose_x(b, m):
                pe.wait_ge(ln_applied, T * b + m + 1)
                if m == 0:
                    wait(pe, v_copied, T * b)
                    wait(pe, o_added, T * (b - 1))
                elif m == 2:
                    wait(pe, k_low, K * b)
                else:
                    pe.wait_ge(xt_low, T * b + (1 if m == 1 else 2))
                for k in range(K):
                    last = nc.tensor.transpose(proj("x", m)[:, P * k:P * k + P], x_tile(m)[:, P * k:P * k + P], ident[:])
                last.then_inc(xt_done, 1)

            NOW = {0: "v0", 1: "v1 v2", 2: "v3 q2", 4: "k2", 8: "q3", 9: "k3"}
            PREV = {3: "o0", 5: "o1", 6: "o2", 7: "o3"}
            NEXT = {12: "q0", 13: "k0", 14: "q1", 15: "k1"}

            def project(i, s, has_prev, has_next, third):
                pieces = [(i - 1, x) for x in PREV.get(s, "").split()] if has_prev else []
                pieces += [(i, x) for x in NOW.get(s, "").split()]
                if has_next:
                    pieces += [(i + 1, x) for x in NEXT.get(s, "").split()]
                steps = [(b, x, k) for b, x in pieces for k in range(K)]
                shares = (0, 1, 2, 4)
                a, z = (len(steps) * share // 4 for share in shares[third:third + 2])
                for b, x, k in steps[a:z]:
                    n = int(x[1])
                    if x[0] == "q":
                        project_q(b, n, k, has_prev)
                    elif x[0] == "k":
                        project_k(b, n, k)
                    elif x[0] == "v":
                        project_v(b, n, k)
                    else:
                        project_o(b, n, k)

            def iteration(i, has_prev, has_next):
                for s in range(H):
                    before = (i, s - 1) if s > 0 else (i - 1, H - 1)
                    scores(i, s, 0)
                    scores(i, s, 1)
                    project(i, s, has_prev, has_next, 0)
                    if s > 0 or has_prev:
                        transpose_probs(*before, 0)
                    scores(i, s, 2)
                    project(i, s, has_prev, has_next, 1)
                    if s > 0 or has_prev:
                        transpose_probs(*before, 1)
                    if s % HG == 0 and (s > 0 or has_prev):
                        transpose_probs(*before, 2)
                        project(i, s, has_prev, has_next, 2)
                    else:
                        project(i, s, has_prev, has_next, 2)
                        if s > 0 or has_prev:
                            transpose_probs(*before, 2)
                    if 8 <= s <= 10 and has_next:
                        transpose_x(i + 1, s - 8)
                    if s == 10 and has_next:
                        transpose_x(i + 1, 3)
                    if s % HG == 0 and (s > 0 or has_prev):
                        group = (i, s // HG - 1) if s > 0 else (i - 1, K - 1)
                        values(*group)
                        transpose_inverse(*group)

            pe.wait_ge(pool_const, 4)
            for m in range(T):
                transpose_x(0, m)
            pe.wait_ge(w_low, 1)
            for k in range(K):
                project_q(0, 0, k)
            pe.wait_ge(w_low, 2)
            for k in range(K):
                project_k(0, 0, k)
            for k in range(K):
                project_q(0, 1, k)
            for k in range(K):
                project_k(0, 1, k)
            pe.wait_ge(w_low, 3)
            iteration(0, False, True)
            with pe.Fori(1, B - 1) as i:
                iteration(i, True, True)
            iteration(B - 1, True, False)
            for n in range(3):
                transpose_probs(B - 1, H - 1, n)
            values(B - 1, K - 1)
            transpose_inverse(B - 1, K - 1)
            for m in range(T):
                for k in range(K):
                    project_o(B - 1, m, k, False)


def channel_mix_phase(nc, lent, x1, g_ffn, mu_r, mu_k, out):
    B, S, D = x1.shape
    T = S // P
    K = D // P

    with ExitStack() as ctx:
        def sb(name, shape, dt=F32):
            return ctx.enter_context(nc.sbuf_tensor(name, shape, dt))

        def psums(name, n):
            return [ctx.enter_context(nc.psum_tensor(f"{name}{i}", [P, 512], F32)) for i in range(n)]

        def sem(name):
            return ctx.enter_context(nc.semaphore(name))

        def pair(name):
            return [sb(f"{name}_{part}", [P, K, S], F32R) for part in ("high", "low")]

        w = {"k": lent["xT"], "r": lent["cT"], "v": lent["wv"]}
        x_in = lent["wk_room"][1]
        ident = lent["ident"]
        xT = sb("ffn_xT", [P, K, S + 1])
        delta = sb("delta", [P, K, S])
        mixed = {n: sb(f"mixed_{n}", [P, 2, S]) for n in "kr"}
        mix = {n: pair(f"mix_{n}") for n in "kr"}
        relu = sb("relu", [P, 2, S])
        square = sb("square", [P, K, S])
        kact = pair("kact")
        r_tanh = sb("r_tanh", [P, T, D])
        y = sb("y", [P, 2, D])
        res = sb("res", [P, T, D])
        mu = sb("mu", [P, 2, K])
        gate = sb("ffn_gate", [P, 2])
        stats = sb("ffn_stats", [P, T, 6])
        moments = sb("ffn_moments", [P, T, 2])
        newton = sb("ffn_newton", [P, 3, T])

        x_ps, k_ps, r_ps, v_ps = psums("ffn_x_ps", 2), psums("ffn_k_ps", 2), psums("ffn_r_ps", 2), psums("ffn_v_ps", 2)

        sp_turns, pool_turns, dve_turns = sem("ffn_sp_turns"), sem("ffn_pool_turns"), sem("ffn_dve_turns")
        small_loaded, gate_ready = sem("ffn_small"), sem("ffn_gate_ready")
        zeroed = sem("zeroed")
        x_loaded = sem("ffn_x_loaded")
        ln_step = sem("ffn_ln_step")
        bn_done = sem("ffn_bn_done")
        ln_stats = sem("ffn_ln_stats")
        ln_applied = sem("ffn_ln_applied")
        xt_done = sem("ffn_xt_done")
        xt_copied = sem("ffn_xt_copied")
        delta_done = sem("delta_done")
        mixed_done = {n: sem(f"mixed_{n}_done") for n in "kr"}
        mix_high = {n: sem(f"mix_{n}_high") for n in "kr"}
        mix_low = {n: sem(f"mix_{n}_low") for n in "kr"}
        k_done, r_done, v_done = sem("ffn_k_done"), sem("ffn_r_done"), sem("ffn_v_done")
        relu_done, square_done = sem("relu_done"), sem("square_done")
        kact_high, kact_low = sem("kact_high"), sem("kact_low")
        r_ready = sem("r_ready")
        y_done, added = sem("y_done"), sem("added")
        res_loaded = [sem(f"ffn_res_loaded{m}") for m in range(T)]
        stored = [sem(f"ffn_stored{m}") for m in range(T)]

        block = ctx.enter_context(nc.Block())

        @block.sync
        def _(sp):
            def load_x(b):
                wait(sp, xt_done, T * b)
                stand_alone(sp, sp_turns, b)
                sp.dma_start(x_in[:], x1[b].rearrange("(t p) d -> p t d", p=P)).then_inc(x_loaded, 16)

            def load_res(b, m):
                wait(sp, stored[m], 16 * b)
                stand_alone(sp, sp_turns, b)
                sp.dma_start(res[:, m, :], x1[b, P * m:P * m + P]).then_inc(res_loaded[m], 16)

            def store(b, m):
                sp.wait_ge(added, T * b + m + 1)
                stand_alone(sp, sp_turns, b)
                sp.dma_start(out[b, P * m:P * m + P], res[:, m, :]).then_inc(stored[m], 16)

            def iteration(i, has_next_but_one):
                for m in range(T):
                    load_res(i, m)
                if has_next_but_one:
                    load_x(i + 2)
                for m in range(T):
                    store(i, m)

            sp.dma_start(mu[:, 0, :], mu_k).then_inc(small_loaded, 16)
            sp.dma_start(mu[:, 1, :], mu_r).then_inc(small_loaded, 16)
            sp.dma_start(gate[:, 0:1], g_ffn.partition_broadcast(P)).then_inc(small_loaded, 16)
            load_x(1)
            iteration(0, True)
            with sp.Fori(1, B - 2) as i:
                iteration(i, True)
            iteration(B - 2, False)
            iteration(B - 1, False)
            for m in range(T):
                sp.wait_ge(stored[m], 16 * B)

        @block.gpsimd
        def _(pool):
            def apply_layernorm(b, m):
                nc.gpsimd.tensor_scalar(x_in[:, m, :], x_in[:, m, :], moments[:, m, 0:1], newton[:, 1, m:m + 1],
                                        ALU.subtract, ALU.mult).then_inc(ln_applied, 1)

            def layernorm(b):
                pool.wait_ge(ln_stats, T * b)
                invert_deviation(nc, pool, b - 1, moments[:, :, 1], newton, ln_step, pool_turns)
                stand_alone(pool, pool_turns, b)
                for m in range(T):
                    apply_layernorm(b, m)

            def take_delta(b, k):
                pool.wait_ge(xt_copied, T * (b + 1))
                wait(pool, mixed_done["r"], K * b)
                nc.gpsimd.tensor_tensor(delta[:, k, :], xT[:, k, 1:S + 1], xT[:, k, 0:S], ALU.subtract).then_inc(delta_done, 1)

            def low_part_act(b, k):
                pool.wait_ge(kact_high, K * b + k + 1)
                nc.gpsimd.tensor_tensor(kact[1][:, k, :], square[:, k, :], kact[0][:, k, :].bitcast(F32),
                                        ALU.subtract).then_inc(kact_low, 1)

            def iteration(i, has_next, has_next_but_one):
                low_part_act(i, 0)
                if has_next:
                    for k in range(K):
                        take_delta(i + 1, k)
                for k in range(1, K):
                    low_part_act(i, k)
                if has_next_but_one:
                    layernorm(i + 2)

            pool.wait_ge(zeroed, 1)
            for k in range(K):
                take_delta(0, k)
            pool.wait_ge(ln_stats, T)
            invert_deviation(nc, pool, 0, moments[:, :, 1], newton, ln_step, pool_turns)
            iteration(0, True, True)
            with pool.Fori(1, B - 2) as i:
                iteration(i, True, True)
            iteration(B - 2, True, False)
            iteration(B - 1, False, False)

        @block.scalar
        def _(act):
            def copy_x(b, m):
                act.wait_ge(xt_done, T * b + m + 1)
                wait(act, mixed_done["r"], K * b)
                nc.scalar.copy(xT[:, :, 1 + P * m:1 + P * m + P], x_ps[m % 2][:].rearrange("p (k n) -> p k n", k=K)
                               ).then_inc(xt_copied, 1)

            def high_part_mix(b, n, k, done):
                act.wait_ge(mixed_done[n], K * b + k + 1)
                wait(act, done, K * b)
                nc.scalar.copy(mix[n][0][:, k, :], mixed[n][:, k % 2, :]).then_inc(mix_high[n], 1)

            def relu_k(b, k):
                act.wait_ge(k_done, K * b + k + 1)
                wait(act, square_done, K * b + k - 1)
                nc.scalar.activation(relu[:, k % 2, :], k_ps[k % 2][:], ACT.Relu).then_inc(relu_done, 1)

            def high_part_act(b, k):
                act.wait_ge(square_done, K * b + k + 1)
                wait(act, v_done, T * b)
                nc.scalar.copy(kact[0][:, k, :], square[:, k, :]).then_inc(kact_high, 1)

            def gate_r(b, m):
                act.wait_ge(r_done, T * b + m + 1)
                wait(act, y_done, T * (b - 1) + m + 1)
                nc.scalar.activation(r_tanh[:, m, :], r_ps[m % 2][:], ACT.Tanh, scale=0.5).then_inc(r_ready, 1)

            def iteration(i, has_next):
                relu_k(i, 0)
                if has_next:
                    copy_x(i + 1, 0)
                    copy_x(i + 1, 1)
                relu_k(i, 1)
                high_part_act(i, 0)
                if has_next:
                    copy_x(i + 1, 2)
                    copy_x(i + 1, 3)
                relu_k(i, 2)
                high_part_act(i, 1)
                relu_k(i, 3)
                high_part_act(i, 2)
                high_part_act(i, 3)
                gate_r(i, 0)
                if has_next:
                    high_part_mix(i + 1, "k", 0, k_done)
                    high_part_mix(i + 1, "k", 1, k_done)
                gate_r(i, 1)
                if has_next:
                    high_part_mix(i + 1, "k", 2, k_done)
                    high_part_mix(i + 1, "k", 3, k_done)
                gate_r(i, 2)
                gate_r(i, 3)
                if has_next:
                    for k in range(K):
                        high_part_mix(i + 1, "r", k, r_done)

            for m in range(T):
                copy_x(0, m)
            for n, done in (("k", k_done), ("r", r_done)):
                for k in range(K):
                    high_part_mix(0, n, k, done)
            act.wait_ge(small_loaded, 16 * 3)
            nc.scalar.activation(gate[:, 1:2], gate[:, 0:1], ACT.Tanh).then_inc(gate_ready, 1)
            iteration(0, True)
            with act.Fori(1, B - 1) as i:
                iteration(i, True)
            iteration(B - 1, False)

        @block.vector
        def _(dve):
            def layernorm_stats(b):
                dve.wait_ge(x_loaded, 16 * b)
                wait(dve, ln_stats, T * (b - 1))
                for m in range(T):
                    nc.vector.bn_stats(stats[:, m, :], x_in[:, m, :]).then_inc(bn_done, 1)
                dve.wait_ge(bn_done, T * b)
                wait(dve, ln_applied, T * (b - 1))
                stand_alone(dve, dve_turns, b)
                for m in range(T):
                    nc.vector.bn_aggr(moments[:, m, :], stats[:, m, :]).then_inc(ln_stats, 1)

            def mix_tokens(b, n, k):
                dve.wait_ge(delta_done, K * b + k + 1)
                wait(dve, mix_low[n], K * b + k - 1)
                col = "kr".index(n)
                nc.vector.scalar_tensor_tensor(out=mixed[n][:, k % 2, :], in0=delta[:, k, :], scalar=mu[:, col, k:k + 1],
                                               in1=xT[:, k, 0:S], op0=ALU.mult, op1=ALU.add).then_inc(mixed_done[n], 1)

            def low_part_mix(b, n, k):
                dve.wait_ge(mix_high[n], K * b + k + 1)
                nc.vector.tensor_tensor(mix[n][1][:, k, :], mixed[n][:, k % 2, :], mix[n][0][:, k, :].bitcast(F32),
                                        ALU.subtract).then_inc(mix_low[n], 1)

            def mix_all(b, n):
                mix_tokens(b, n, 0)
                for k in range(1, K):
                    mix_tokens(b, n, k)
                    low_part_mix(b, n, k - 1)
                low_part_mix(b, n, K - 1)

            def square_k(b, k):
                dve.wait_ge(relu_done, K * b + k + 1)
                wait(dve, kact_low, K * (b - 1) + k + 1)
                nc.vector.scalar_tensor_tensor(out=square[:, k, :], in0=k_ps[k % 2][:], scalar=0.0,
                                               in1=relu[:, k % 2, :], op0=ALU.max, op1=ALU.mult).then_inc(square_done, 1)

            def combine(b, m):
                dve.wait_ge(v_done, T * b + m + 1)
                dve.wait_ge(r_ready, T * b + m + 1)
                wait(dve, added, T * b + m - 1)
                nc.vector.scalar_tensor_tensor(out=y[:, m % 2, :], in0=r_tanh[:, m, :], scalar=1.0, in1=v_ps[m % 2][:],
                                               op0=ALU.add, op1=ALU.mult).then_inc(y_done, 1)
                dve.wait_ge(y_done, T * b + m + 1)
                dve.wait_ge(res_loaded[m], 16 * (b + 1))
                nc.vector.scalar_tensor_tensor(out=res[:, m, :], in0=y[:, m % 2, :], scalar=gate[:, 0:1], in1=res[:, m, :],
                                               op0=ALU.mult, op1=ALU.add).then_inc(added, 1)

            def iteration(i, has_next, has_next_but_one):
                for k in range(K):
                    square_k(i, k)
                if has_next_but_one:
                    layernorm_stats(i + 2)
                if has_next:
                    mix_all(i + 1, "k")
                    mix_tokens(i + 1, "r", 0)
                    for k in range(1, K):
                        mix_tokens(i + 1, "r", k)
                        low_part_mix(i + 1, "r", k - 1)
                        combine(i, k - 1)
                    low_part_mix(i + 1, "r", K - 1)
                    combine(i, K - 1)
                else:
                    for m in range(T):
                        combine(i, m)

            nc.vector.memset(xT[:, :, 0:1], 0.0).then_inc(zeroed, 1)
            dve.wait_ge(small_loaded, 16 * 3)
            dve.wait_ge(zeroed, 1)
            mix_all(0, "k")
            layernorm_stats(1)
            mix_all(0, "r")
            dve.wait_ge(ln_step, LN_STEPS)
            for m in range(T):
                nc.vector.tensor_scalar(x_in[:, m, :], x_in[:, m, :], moments[:, m, 0:1], newton[:, 1, m:m + 1],
                                        ALU.subtract, ALU.mult).then_inc(ln_applied, 1)
            dve.wait_ge(gate_ready, 1)
            nc.vector.tensor_scalar(gate[:, 0:1], gate[:, 1:2], 0.5, None, ALU.mult).then_inc(zeroed, 1)
            dve.wait_ge(zeroed, 2)
            iteration(0, True, True)
            with dve.Fori(1, B - 2) as i:
                iteration(i, True, True)
            iteration(B - 2, True, False)
            iteration(B - 1, False, False)

        @block.tensor
        def _(pe):
            def transpose_x(b, m):
                wait(pe, ln_applied, T * (b - 1) + m + 1)
                wait(pe, xt_copied, T * b + m - 1)
                for k in range(K):
                    last = nc.tensor.transpose(x_ps[m % 2][:, P * k:P * k + P], x_in[:, m, P * k:P * k + P], ident[:])
                last.then_inc(xt_done, 1)

            def project_k(b, g):
                if g == 0:
                    pe.wait_ge(mix_low["k"], K * (b + 1))
                wait(pe, square_done, K * b + g - 1)
                exact_product(nc, k_ps[g % 2][:], lambda k: [part[:, k, P * g:P * g + P] for part in w["k"]],
                              lambda k: [part[:, k, :] for part in mix["k"]], range(K)).then_inc(k_done, 1)

            def project_r(b, m):
                if m == 0:
                    pe.wait_ge(mix_low["r"], K * (b + 1))
                wait(pe, r_ready, T * b + m - 1)
                exact_product(nc, r_ps[m % 2][:], lambda k: [part[:, k, P * m:P * m + P] for part in mix["r"]],
                              lambda k: [part[:, k, :] for part in w["r"]], range(K)).then_inc(r_done, 1)

            def project_v(b, m):
                if m == 0:
                    pe.wait_ge(kact_low, K * (b + 1))
                wait(pe, y_done, T * b + m - 1)
                exact_product(nc, v_ps[m % 2][:], lambda k: [part[:, k, P * m:P * m + P] for part in kact],
                              lambda k: [part[:, k, :] for part in w["v"]], range(K)).then_inc(v_done, 1)

            def iteration(i, has_next):
                for g in range(K):
                    project_k(i, g)
                    if has_next and g < T // 2:
                        transpose_x(i + 1, 2 * g)
                        transpose_x(i + 1, 2 * g + 1)
                for m in range(T):
                    project_r(i, m)
                for m in range(T):
                    project_v(i, m)

            for m in range(T):
                transpose_x(0, m)
            iteration(0, True)
            with pe.Fori(1, B - 1) as i:
                iteration(i, True)
            iteration(B - 1, False)


def build(nc, x, ctxT, mask, g_xattn, g_ffn, wqT, bq, wkT, bk, wvT, bv, woT, bo, w_rT, w_kT, w_vT, mu_r, mu_k, out):
    x1 = nc.dram_tensor("x1", list(x.shape), F32, kind="Internal").ap()
    with ExitStack() as ctx:
        shape = [P, x.shape[2] // P, x.shape[1]]
        lent = {}
        for n in ("wq", "wk", "wv", "xT", "cT"):
            rooms = [shared_room(nc, ctx, f"{n}_{part}", shape) for part in ("high", "low")]
            lent[n], lent[f"{n}_room"] = zip(*rooms)
        lent["ident"] = ctx.enter_context(nc.sbuf_tensor("ident", [P, P], F32))
        ffn_wT = {"k": w_kT, "r": w_rT, "v": w_vT}
        attention_phase(nc, lent, x, ctxT, mask, g_xattn, wqT, bq, wkT, bk, wvT, bv, woT, bo, x1, ffn_wT)
        channel_mix_phase(nc, lent, x1, g_ffn, mu_r, mu_k, out)


def lay_out(inputs):
    a = {n: np.asarray(v) for n, v in inputs.items()}
    D = a["x"].shape[-1]
    K, DH = D // P, D // HEADS

    def tiles(w):
        return np.ascontiguousarray(w.T.reshape(K, P, -1).transpose(1, 0, 2))

    def head_interleaved(v):
        return v.reshape(K, P // DH, DH, -1).swapaxes(1, 2).reshape(D, -1)

    def columns(v):
        return np.ascontiguousarray(v.reshape(K, P).T)

    return {
        "x": np.ascontiguousarray(a["x"]),
        "ctxT": np.ascontiguousarray(a["ctx_1024"].transpose(0, 2, 1)),
        "mask": np.ascontiguousarray(a["mask_BxS2_if1"]),
        "g_xattn": np.ascontiguousarray(a["g_xattn"]),
        "g_ffn": np.ascontiguousarray(a["g_ffn"]),
        "wqT": tiles(head_interleaved(a["L0_xattn_Wq"])),
        "bq": columns(head_interleaved(a["L0_xattn_bq"])),
        "wkT": tiles(head_interleaved(a["L0_xattn_Wk"])),
        "bk": columns(head_interleaved(a["L0_xattn_bk"])),
        "wvT": tiles(a["L0_xattn_Wv"]),
        "bv": columns(a["L0_xattn_bv"]),
        "woT": tiles(a["L0_xattn_Wo"]),
        "bo": np.ascontiguousarray(a["L0_xattn_bo"]),
        "w_rT": tiles(a["L0_ffn_W_r"]),
        "w_kT": tiles(a["L0_ffn_W_k"]),
        "w_vT": tiles(a["L0_ffn_W_v"]),
        "mu_r": columns(a["L0_ffn_mu_r"]),
        "mu_k": columns(a["L0_ffn_mu_k"]),
    }


def kernel(**inputs):
    import concourse.bacc as bacc
    from concourse.bass_utils import run_bass_kernel_spmd

    arrays = lay_out(inputs)
    nc = bacc.Bacc("TRN2", target_bir_lowering=False, num_devices=1)
    args = {n: nc.dram_tensor(f"in_{n}", v.shape, mybir.dt.from_np(v.dtype), kind="ExternalInput").ap()
            for n, v in arrays.items()}
    out = nc.dram_tensor("out_x", arrays["x"].shape, F32, kind="ExternalOutput").ap()
    build(nc, **args, out=out)
    run = run_bass_kernel_spmd(nc, [{f"in_{n}": v for n, v in arrays.items()}], core_ids=[0])
    return run.results[0]["out_x"]
```
